# Optimizing a Trainium2 kernel written in Bass

```python
import numpy as np
import jax
import jax.numpy as jnp

def _softmax(x, axis=-1):
    return jax.nn.softmax(x, axis=axis)

def _gelu(x):
    return jax.nn.gelu(x, approximate=True)

def _silu(x):
    return jax.nn.silu(x)

def _sigmoid(x):
    return jax.nn.sigmoid(x)

def _layernorm(x, axis=-1, eps=1e-05):
    m = jnp.mean(x, axis=axis, keepdims=True)
    v = jnp.var(x, axis=axis, keepdims=True)
    return (x - m) / jnp.sqrt(v + eps)

def _scatter_add(tgt, idx, src, axis=0):
    return tgt.at[idx].add(src)

def _segment_sum(src, seg, n):
    return jax.ops.segment_sum(src, seg, n)
kernel_name = 'mk_early_fusion_d2_tok_img1024_r4_8a9f63'

def setup_inputs(seed: int=0):
    np.random.seed(seed)
    _w = jnp.asarray

    def _rec_inputs():
        import jax
        import jax.numpy as jnp
        _rk = jax.random.key(seed)
        x = -0.00016672 + 0.999947 * jax.random.normal(jax.random.fold_in(_rk, 1), (32, 3, 96, 96), jnp.float32)
        txt = -0.000196989 + 0.577976 * jax.random.normal(jax.random.fold_in(_rk, 2), (32, 32, 256), jnp.float32)
        return (x, txt)
    x, txt = _rec_inputs()

    def _L0_tok_setup():
        import jax, jax.numpy as jnp
        import numpy as np
        PATCH = 16
        D_MODEL = 256

        def patchify(imgs, p):
            n, c, H, W = imgs.shape
            h, w = (H // p, W // p)
            x = imgs.reshape(n, c, h, p, w, p)
            x = jnp.einsum('nchpwq->nhwpqc', x)
            return x.reshape(n, h * w, p * p * c)
        key = jax.random.key(seed)
        k1, k2, k3 = jax.random.split(key, 3)
        val = jax.random.normal(k1, (64, 3, 96, 96), dtype=jnp.float32)
        in_dim = PATCH * PATCH * 3
        bound = 1.0 / np.sqrt(in_dim)
        W = jax.random.uniform(k2, (D_MODEL, in_dim), dtype=jnp.float32, minval=-bound, maxval=bound)
        b = jax.random.uniform(k3, (D_MODEL,), dtype=jnp.float32, minval=-bound, maxval=bound)
        return {'val': val, 'W': W, 'b': b}
    _L0_tok_all = _L0_tok_setup()
    _L0_tok_in = {k: v for k, v in _L0_tok_all.items() if k in ('W', 'b')}
    del _L0_tok_all

    def _L0_attn_setup():
        import jax, jax.numpy as jnp
        import numpy as np
        D_MODEL = 256
        N_HEADS = 16
        WINDOW = 64
        SEQ = 1024
        BATCH = 1
        NEG_INF = -1e+30
        key = jax.random.key(seed)
        ks = jax.random.split(key, 5)
        scale = 0.02
        inp = {'x': jax.random.normal(ks[0], (BATCH, SEQ, D_MODEL), jnp.float32)}
        for i, name in enumerate(['Wq', 'Wk', 'Wv', 'Wo']):
            inp[name] = jax.random.normal(ks[1 + i], (D_MODEL, D_MODEL), jnp.float32) * scale
        for name in ['bq', 'bk', 'bv', 'bo']:
            inp[name] = jnp.zeros((D_MODEL,), jnp.float32)
        return inp
    _L0_attn_all = _L0_attn_setup()
    _L0_attn_in = {k: v for k, v in _L0_attn_all.items() if k in ('Wq', 'bq', 'Wk', 'bk', 'Wv', 'bv', 'Wo', 'bo')}
    del _L0_attn_all

    def _L0_ffn_setup():
        import jax, jax.numpy as jnp
        import numpy as np
        H = 256
        I = 128
        E = 64
        G = 8
        TOPK_GROUP = 4
        K = 8
        I_SH = 256
        SCALE = 2.5

        def _route(x, router_w, e_bias):
            T = x.shape[0]
            scores = jax.nn.sigmoid(x.astype(jnp.float32) @ router_w.T.astype(jnp.float32))
            sfc = jax.lax.stop_gradient(scores) + e_bias[None, :]
            group_scores = jax.lax.top_k(sfc.reshape(T, G, E // G), 2)[0].sum(-1)
            _, gidx = jax.lax.top_k(group_scores, TOPK_GROUP)
            gmask = jax.nn.one_hot(gidx, G, dtype=sfc.dtype).sum(1)
            smask = jnp.repeat(gmask, E // G, axis=1)
            masked = jnp.where(smask > 0, sfc, 0.0)
            _, topk_idx = jax.lax.top_k(masked, K)
            w = jnp.take_along_axis(scores, topk_idx, axis=1)
            w = w / (w.sum(-1, keepdims=True) + 1e-20)
            return (topk_idx, w * SCALE)
        key = jax.random.key(seed)
        ks = jax.random.split(key, 9)
        s = 0.02
        return {'hidden_states': jax.random.normal(ks[0], (2, 256, H), jnp.float32), 'router_w': jax.random.normal(ks[1], (E, H), jnp.float32) * s, 'e_bias': jnp.zeros((E,), jnp.float32), 'Wg': jax.random.normal(ks[2], (E, H, I), jnp.float32) * s, 'Wu': jax.random.normal(ks[3], (E, H, I), jnp.float32) * s, 'Wd': jax.random.normal(ks[4], (E, I, H), jnp.float32) * s, 'SWg': jax.random.normal(ks[5], (H, I_SH), jnp.float32) * s, 'SWu': jax.random.normal(ks[6], (H, I_SH), jnp.float32) * s, 'SWd': jax.random.normal(ks[7], (I_SH, H), jnp.float32) * s}
    _L0_ffn_all = _L0_ffn_setup()
    _L0_ffn_in = {k: v for k, v in _L0_ffn_all.items() if k in ('router_w', 'e_bias', 'Wg', 'Wu', 'Wd', 'SWg', 'SWu', 'SWd')}
    del _L0_ffn_all

    def _L1_attn_setup():
        import jax, jax.numpy as jnp
        import numpy as np
        EMBED_DIM = 256
        NUM_HEADS = 16
        HEAD_DIM = EMBED_DIM // NUM_HEADS
        SCALING = HEAD_DIM ** (-0.5)
        key = jax.random.key(seed)
        k1, k2, k3, k4, k5 = jax.random.split(key, 5)
        B, S, E, H = (2, 512, EMBED_DIM, NUM_HEADS)
        x = jax.random.normal(k1, (B, S, E), dtype=jnp.float32)
        W_A = jax.random.normal(k2, (H, E), dtype=jnp.float32) * E ** (-0.5)
        W_V = jax.random.normal(k3, (E, E), dtype=jnp.float32) * E ** (-0.5)
        W_O = jax.random.normal(k4, (E, E), dtype=jnp.float32) * E ** (-0.5)
        b_O = jax.random.normal(k5, (E,), dtype=jnp.float32) * 0.01
        return {'x': x, 'W_A': W_A, 'W_V': W_V, 'W_O': W_O, 'b_O': b_O}
    _L1_attn_all = _L1_attn_setup()
    _L1_attn_in = {k: v for k, v in _L1_attn_all.items() if k in ('W_A', 'W_V', 'W_O', 'b_O')}
    del _L1_attn_all

    def _L1_ffn_setup():
        import jax, jax.numpy as jnp
        import numpy as np
        B, S, D, F, E = (4, 512, 256, 1024, 8)
        key = jax.random.key(seed)
        ks = jax.random.split(key, 7)
        s1 = 1.0 / np.sqrt(D)
        s2 = 1.0 / np.sqrt(F)
        x = jax.random.normal(ks[0], (B, S, D), dtype=jnp.float32)
        W1 = jax.random.uniform(ks[1], (E, D, F), jnp.float32, -s1, s1)
        b1 = jax.random.uniform(ks[2], (E, F), jnp.float32, -s1, s1)
        W2 = jax.random.uniform(ks[3], (E, F, D), jnp.float32, -s2, s2)
        b2 = jax.random.uniform(ks[4], (E, D), jnp.float32, -s2, s2)
        Wr = jax.random.uniform(ks[5], (D, E), jnp.float32, -s1, s1)
        br = jax.random.uniform(ks[6], (E,), jnp.float32, -s1, s1)
        return {'x': x, 'W1': W1, 'b1': b1, 'W2': W2, 'b2': b2, 'Wr': Wr, 'br': br}
    _L1_ffn_all = _L1_ffn_setup()
    _L1_ffn_in = {k: v for k, v in _L1_ffn_all.items() if k in ('W1', 'b1', 'W2', 'b2', 'Wr', 'br')}
    del _L1_ffn_all
    return {'x': x, 'txt': txt, 'L0_tok_W': _L0_tok_in['W'], 'L0_tok_b': _L0_tok_in['b'], 'L0_attn_Wq': _L0_attn_in['Wq'], 'L0_attn_bq': _L0_attn_in['bq'], 'L0_attn_Wk': _L0_attn_in['Wk'], 'L0_attn_bk': _L0_attn_in['bk'], 'L0_attn_Wv': _L0_attn_in['Wv'], 'L0_attn_bv': _L0_attn_in['bv'], 'L0_attn_Wo': _L0_attn_in['Wo'], 'L0_attn_bo': _L0_attn_in['bo'], 'L0_ffn_router_w': _L0_ffn_in['router_w'], 'L0_ffn_e_bias': _L0_ffn_in['e_bias'], 'L0_ffn_Wg': _L0_ffn_in['Wg'], 'L0_ffn_Wu': _L0_ffn_in['Wu'], 'L0_ffn_Wd': _L0_ffn_in['Wd'], 'L0_ffn_SWg': _L0_ffn_in['SWg'], 'L0_ffn_SWu': _L0_ffn_in['SWu'], 'L0_ffn_SWd': _L0_ffn_in['SWd'], 'L1_attn_W_A': _L1_attn_in['W_A'], 'L1_attn_W_V': _L1_attn_in['W_V'], 'L1_attn_W_O': _L1_attn_in['W_O'], 'L1_attn_b_O': _L1_attn_in['b_O'], 'L1_ffn_W1': _L1_ffn_in['W1'], 'L1_ffn_b1': _L1_ffn_in['b1'], 'L1_ffn_W2': _L1_ffn_in['W2'], 'L1_ffn_b2': _L1_ffn_in['b2'], 'L1_ffn_Wr': _L1_ffn_in['Wr'], 'L1_ffn_br': _L1_ffn_in['br']}

def reference(x, txt, L0_tok_W, L0_tok_b, L0_attn_Wq, L0_attn_bq, L0_attn_Wk, L0_attn_bk, L0_attn_Wv, L0_attn_bv, L0_attn_Wo, L0_attn_bo, L0_ffn_router_w, L0_ffn_e_bias, L0_ffn_Wg, L0_ffn_Wu, L0_ffn_Wd, L0_ffn_SWg, L0_ffn_SWu, L0_ffn_SWd, L1_attn_W_A, L1_attn_W_V, L1_attn_W_O, L1_attn_b_O, L1_ffn_W1, L1_ffn_b1, L1_ffn_W2, L1_ffn_b2, L1_ffn_Wr, L1_ffn_br):
    import jax
    import jax.numpy as jnp

    def _L0_tok_ref(val, W, b):
        import jax, jax.numpy as jnp
        import numpy as np
        PATCH = 16
        D_MODEL = 256

        def patchify(imgs, p):
            n, c, H, W = imgs.shape
            h, w = (H // p, W // p)
            x = imgs.reshape(n, c, h, p, w, p)
            x = jnp.einsum('nchpwq->nhwpqc', x)
            return x.reshape(n, h * w, p * p * c)
        patches = patchify(val, PATCH)
        return jnp.einsum('nld,md->nlm', patches, W) + b

    def _L0_attn_ref(x, Wq, bq, Wk, bk, Wv, bv, Wo, bo):
        import jax, jax.numpy as jnp
        import numpy as np
        D_MODEL = 256
        N_HEADS = 16
        WINDOW = 64
        SEQ = 1024
        BATCH = 1
        NEG_INF = -1e+30
        B, S, D = x.shape
        H = N_HEADS
        hd = D // H
        q = (x @ Wq + bq).reshape(B, S, H, hd).transpose(0, 2, 1, 3)
        k = (x @ Wk + bk).reshape(B, S, H, hd).transpose(0, 2, 1, 3)
        v = (x @ Wv + bv).reshape(B, S, H, hd).transpose(0, 2, 1, 3)
        scale = 1.0 / jnp.sqrt(jnp.asarray(hd, x.dtype))
        scores = jnp.einsum('bhqd,bhkd->bhqk', q, k) * scale
        i = jnp.arange(S)[:, None]
        j = jnp.arange(S)[None, :]
        allowed = (j <= i) & (i - j < WINDOW)
        scores = jnp.where(allowed, scores, NEG_INF)
        attn = jax.nn.softmax(scores, axis=-1)
        out = jnp.einsum('bhqk,bhkd->bhqd', attn, v)
        out = out.transpose(0, 2, 1, 3).reshape(B, S, D)
        return out @ Wo + bo

    def _L0_ffn_ref(hidden_states, router_w, e_bias, Wg, Wu, Wd, SWg, SWu, SWd):
        import jax, jax.numpy as jnp
        import numpy as np
        H = 256
        I = 128
        E = 64
        G = 8
        TOPK_GROUP = 4
        K = 8
        I_SH = 256
        SCALE = 2.5

        def _route(x, router_w, e_bias):
            T = x.shape[0]
            scores = jax.nn.sigmoid(x.astype(jnp.float32) @ router_w.T.astype(jnp.float32))
            sfc = jax.lax.stop_gradient(scores) + e_bias[None, :]
            group_scores = jax.lax.top_k(sfc.reshape(T, G, E // G), 2)[0].sum(-1)
            _, gidx = jax.lax.top_k(group_scores, TOPK_GROUP)
            gmask = jax.nn.one_hot(gidx, G, dtype=sfc.dtype).sum(1)
            smask = jnp.repeat(gmask, E // G, axis=1)
            masked = jnp.where(smask > 0, sfc, 0.0)
            _, topk_idx = jax.lax.top_k(masked, K)
            w = jnp.take_along_axis(scores, topk_idx, axis=1)
            w = w / (w.sum(-1, keepdims=True) + 1e-20)
            return (topk_idx, w * SCALE)
        orig_shape = hidden_states.shape
        x = hidden_states.reshape(-1, orig_shape[-1])
        T = x.shape[0]
        topk_idx, topk_w = _route(x, router_w, e_bias)
        coef = jnp.zeros((T, E), topk_w.dtype).at[jnp.arange(T)[:, None], topk_idx].add(topk_w)
        g = jnp.einsum('th,ehi->tei', x, Wg)
        u = jnp.einsum('th,ehi->tei', x, Wu)
        h = jax.nn.silu(g) * u * coef[:, :, None]
        moe_out = jnp.einsum('tei,eih->th', h, Wd)
        shared = jax.nn.silu(x @ SWg) * (x @ SWu) @ SWd
        return (moe_out + shared).reshape(orig_shape)

    def _L1_attn_ref(x, W_A, W_V, W_O, b_O):
        import jax, jax.numpy as jnp
        import numpy as np
        EMBED_DIM = 256
        NUM_HEADS = 16
        HEAD_DIM = EMBED_DIM // NUM_HEADS
        SCALING = HEAD_DIM ** (-0.5)
        B, S, E = x.shape
        H, D = (NUM_HEADS, HEAD_DIM)
        z = jnp.einsum('bse,he->bsh', x, W_A) * SCALING
        z = jax.nn.softmax(z, axis=1)
        zp = jnp.transpose(z, (0, 2, 1))
        i = jnp.arange(S)[:, None]
        j = jnp.arange(S)[None, :]
        idx = (i - j) % S
        tril = (j <= i).astype(x.dtype)
        roll = zp[:, :, idx] * tril
        v = jnp.einsum('bse,fe->bsf', x, W_V).reshape(B, S, H, D)
        out = jnp.einsum('bhij,bjhd->bihd', roll, v).reshape(B, S, E)
        return jnp.einsum('bse,fe->bsf', out, W_O) + b_O

    def _L1_ffn_ref(x, W1, b1, W2, b2, Wr, br):
        import jax, jax.numpy as jnp
        import numpy as np
        B, S, D, F, E = (4, 512, 256, 1024, 8)
        b, s, d = x.shape
        e = Wr.shape[1]
        logits = x @ Wr + br
        idx = jnp.argmax(logits, axis=-1)
        probs = jax.nn.softmax(logits, axis=-1)
        gates = jnp.take_along_axis(probs, idx[..., None], axis=-1)[..., 0]
        xf = x.reshape(-1, d)
        idxf = idx.reshape(-1)
        gf = gates.reshape(-1)
        out = jnp.zeros_like(xf)
        for ei in range(e):
            h = jax.nn.gelu(xf @ W1[ei] + b1[ei], approximate=False)
            y = h @ W2[ei] + b2[ei]
            mask = (idxf == ei).astype(xf.dtype)
            out = out + y * (gf * mask)[:, None]
        return out.reshape(b, s, d)
    h = _L0_tok_ref(x, L0_tok_W, L0_tok_b)
    h = jnp.concatenate([h, txt], axis=1)
    h = h + _L0_attn_ref(_layernorm(h, axis=-1), L0_attn_Wq, L0_attn_bq, L0_attn_Wk, L0_attn_bk, L0_attn_Wv, L0_attn_bv, L0_attn_Wo, L0_attn_bo)
    h = h + _L0_ffn_ref(_layernorm(h, axis=-1), L0_ffn_router_w, L0_ffn_e_bias, L0_ffn_Wg, L0_ffn_Wu, L0_ffn_Wd, L0_ffn_SWg, L0_ffn_SWu, L0_ffn_SWd)
    h = h + _L1_attn_ref(_layernorm(h, axis=-1), L1_attn_W_A, L1_attn_W_V, L1_attn_W_O, L1_attn_b_O)
    h = h + _L1_ffn_ref(_layernorm(h, axis=-1), L1_ffn_W1, L1_ffn_b1, L1_ffn_W2, L1_ffn_b2, L1_ffn_Wr, L1_ffn_br)
    return h

_drawn_inputs = setup_inputs


def setup_inputs(seed=0):
    import zlib

    import numpy as np

    out = dict(_drawn_inputs(seed))
    spreads = {'L0_attn_bq': (0.0, 0.8),
     'L0_attn_bk': (0.0, 0.8),
     'L0_attn_bv': (0.0, 0.1),
     'L0_attn_bo': (0.0, 0.1),
     'L0_ffn_e_bias': (0.0, 0.391)}
    factors = {'L0_attn_Wq': 8.0,
     'L0_attn_Wk': 8.0,
     'L0_ffn_router_w': 3.403,
     'L0_ffn_Wg': 2.839,
     'L0_ffn_Wu': 2.828,
     'L0_ffn_Wd': 2.782,
     'L1_attn_b_O': 3.092,
     'L1_ffn_b1': 8.0,
     'L1_ffn_b2': 7.421,
     'L1_ffn_br': 2.724}
    for name, (base, spread) in spreads.items():
        noise = np.random.default_rng([zlib.crc32(name.encode()), seed]).standard_normal(out[name].shape)
        drawn = base * np.exp(spread * noise) if base else spread * noise
        out[name] = jnp.asarray(drawn.astype(out[name].dtype))
    for name, factor in factors.items():
        out[name] = (out[name] * factor).astype(out[name].dtype)
    return out
```

```python
import concourse.bass as bass
from concourse import mybir
from contextlib import ExitStack
import numpy as np

P = 128
D = 256
DC = D // P
B = 32
NPATCH = 36
NTXT = 32
S = NPATCH + NTXT
T = B * S
NT = T // P
PIN = 768
PC = PIN // P
H = 16
HD = D // H
HC = H // DC
WINDOW = 64
NEG = -1e30
EPS = 1e-5
E0, K0, I0 = 64, 8, 128
G0, KG = 8, 4
SCALE0 = 2.5
REPLACED = -3e38
E1, F1 = 8, 1024
FC1 = F1 // P
SLOTS0 = ((T * K0 + E0 * (P - 1)) // P + 7) // 8 * 8
SLOTS1 = ((T + E1 * (P - 1)) // P + 1) // 2 * 2
NDFT = 2 * S - 1
NF = S
TOK0 = T // 2
EBLK = 8
ABLK = 4
UNITS = ABLK * DC

fp32 = mybir.dt.float32
bf16 = mybir.dt.bfloat16
fp16 = mybir.dt.float16
i32 = mybir.dt.int32
u32 = mybir.dt.uint32
ALU = mybir.AluOpType
ACT = mybir.ActivationFunctionType
AX = mybir.AxisListType


def constants():
    f = np.arange(NF)[None, :]
    j = np.arange(S)[:, None]
    turn = 2 * np.pi * (f * j % NDFT) / NDFT
    weight = np.where(np.arange(NF) == 0, 1.0, 2.0)[:, None] / NDFT
    q = np.arange(S)[:, None]
    k = np.arange(S)[None, :]
    p = np.arange(P)[:, None]
    g = np.arange(G0)
    parts = {
        "ident": np.eye(P),
        "before": (p < np.arange(P)[None, :]) * 1.0,
        "iota": np.tile(np.arange(SLOTS0)[None, :], (P, 1)),
        "token": p + P * np.arange(NT)[None, :] - TOK0,
        "slot_tile": p + P * np.arange(2)[None, :],
        "group_before": np.tile((g[None, :] < g[:, None]).reshape(1, -1) * 1.0, (P, 1)),
        "head_of": (p // HD == np.arange(HC)[None, :]) * 1.0,
        "down_from": np.tile(E1 - np.arange(E1)[None, :], (P, 1)),
        "mask": np.where((k <= q) & (q - k < WINDOW), 0.0, NEG),
        "fwd_re": np.cos(turn),
        "fwd_im": -np.sin(turn),
        "inv_re": (np.cos(turn).T * weight),
        "inv_im": (-np.sin(turn).T * weight),
    }
    at, cols = {}, 0
    for name, a in parts.items():
        at[name] = (cols, a.shape[0], a.shape[1])
        cols += a.shape[1]
    table = np.zeros((P, cols), np.float32)
    for name, a in parts.items():
        c, r, n = at[name]
        table[:r, c:c + n] = a
    return table, at


def early_fusion(nc, a, out, upto=99):
    ctx = ExitStack()
    with ctx:
        k = {}

        def sb(name, shape, dt=fp32, stack=ctx):
            return stack.enter_context(nc.sbuf_tensor(name, shape, dt))

        h = sb("h", [P, NT, D])
        xn = sb("xn", [P, NT, D])
        xT = sb("xT", [P, DC, T])
        _, at = constants()
        cst = sb("cst", [P, a["consts"].shape[1]])
        k.update(stage_sems=[], h=h, xn=xn, xT=xT, cst=cst, sb=sb)

        def const(name, cols=None):
            c, r, n = at[name]
            return cst[0:r, c:c + (cols or n)]

        k["const"] = const
        embed(nc, a, k)
        stages = [
            lambda: layer_norm(nc, k, "n1"),
            lambda: window_attention(nc, a, k),
            lambda: layer_norm(nc, k, "n2"),
            lambda: mixture_0(nc, a, k),
            lambda: layer_norm(nc, k, "n3"),
            lambda: roll_attention(nc, a, k),
            lambda: layer_norm(nc, k, "n4"),
            lambda: mixture_1(nc, a, k),
        ]
        for n, stage in enumerate(stages):
            if n < upto:
                stage()
            if n == 3:
                clear_sems(nc, k)
        store(nc, k, out)


def sems(nc, k, prefix, names):
    made = [nc.alloc_semaphore(f"{prefix}_{n}") for n in names.split()]
    k["stage_sems"] += made
    return made


def ring_sems(nc, k, name, n):
    return sems(nc, k, name, " ".join(str(i) for i in range(n)))


def clear_sems(nc, k):
    nc.clear_and_free_semaphores(k["stage_sems"])
    nc.all_engine_barrier()
    k["stage_sems"] = []


def embed(nc, a, k):
    h, cst = k["h"], k["cst"]
    NB = B // EBLK
    COLS = EBLK * NPATCH
    with ExitStack() as st:
        sb = lambda n, s, d=fp32: k["sb"](n, s, d, st)
        patches = sb("patches", [P, PC, B * NPATCH])
        w = sb("tok_w", [P, PC, D])
        bias = sb("tok_bias", [P, DC])
        txt = sb("txt_cols", [P, DC, B * NTXT])
        hT = sb("hT", [P, DC, B, S])
        ps = st.enter_context(nc.psum_tensor("emb_ps", [P, 4, 512], fp32))
        pt = st.enter_context(nc.psum_tensor("emb_pt", [P, 4, 512], fp32))
        (consts_in, w_in, txt_in, sums, moved, txt_placed, turned, placed) = sems(
            nc, k, "emb", "consts_in w_in txt_in sums moved txt_placed turned placed")
        patches_in = ring_sems(nc, k, "emb_patches", NB)
        hflat = hT[:, :, :, :].rearrange("p c b s -> p c (b s)")
        ident = k["const"]("ident")
        with nc.Block() as block:

            @block.sync
            def _(sp):
                sp.dma_start(w[:, :, :], a["tok_w"]).then_inc(w_in, 16)
                for i in range(NB):
                    sp.dma_start(patches[:, :, i * COLS:(i + 1) * COLS],
                                 a["patches"][:, :, i * COLS:(i + 1) * COLS]).then_inc(patches_in[i], 16)
                sp.dma_start(cst[:, :], a["consts"]).then_inc(consts_in, 16)

            @block.scalar
            def _(act):
                act.dma_start(bias[:, :], a["tok_b"]).then_inc(w_in, 16)
                act.dma_start(txt[:, :, :], a["txt"]).then_inc(txt_in, 16)
                act.wait_ge(w_in, 32)
                for i in range(NB):
                    for m in range(DC):
                        n = i * DC + m
                        act.wait_ge(sums, n + 1)
                        nc.scalar.activation(
                            hT[:, m, i * EBLK:(i + 1) * EBLK, 0:NPATCH],
                            ps[:, n % 4, 0:COLS].rearrange("p (b s) -> p b s", s=NPATCH),
                            ACT.Identity, bias=bias[:, m:m + 1]).then_inc(moved, 1)

            @block.gpsimd
            def _(pool):
                pool.wait_ge(txt_in, 16)
                for m in range(DC):
                    nc.gpsimd.tensor_copy(hT[:, m, :, NPATCH:S],
                                          txt[:, m, :].rearrange("p (b s) -> p b s", s=NTXT)).then_inc(txt_placed, 1)

            @block.tensor
            def _(pe):
                pe.wait_ge(w_in, 32)
                for i in range(NB):
                    pe.wait_ge(patches_in[i], 16)
                    for m in range(DC):
                        n = i * DC + m
                        if n >= 4:
                            pe.wait_ge(moved, n - 3)
                        for c in range(PC):
                            mm = nc.tensor.matmul(ps[:, n % 4, 0:COLS], w[:, c, m * P:(m + 1) * P],
                                                  patches[:, c, i * COLS:(i + 1) * COLS],
                                                  start=(c == 0), stop=(c == PC - 1))
                        mm.then_inc(sums, 1)
                pe.wait_ge(moved, NB * DC)
                pe.wait_ge(txt_placed, DC)
                pe.wait_ge(consts_in, 16)
                for t in range(NT):
                    if t >= 4:
                        pe.wait_ge(placed, t - 3)
                    for c in range(DC):
                        mm = nc.tensor.transpose(pt[:, t % 4, c * P:(c + 1) * P],
                                                 hflat[:, c, t * P:(t + 1) * P], ident)
                    mm.then_inc(turned, 1)

            @block.vector
            def _(dve):
                for t in range(NT):
                    dve.wait_ge(turned, t + 1)
                    nc.vector.tensor_copy(h[:, t, :], pt[:, t % 4, 0:D]).then_inc(placed, 1)


def layer_norm(nc, k, name):
    h, xn, xT = k["h"], k["xn"], k["xT"]
    ident = k["const"]("ident")
    with ExitStack() as st:
        sb = lambda n, s, d=fp32: k["sb"](f"{name}_{n}", s, d, st)
        stats = sb("stats", [P, NT, 6])
        mv = sb("mv", [P, NT, 2])
        eps = sb("eps", [P, 1])
        std = sb("std", [P, NT])
        rstd = sb("rstd", [P, NT])
        pt = st.enter_context(nc.psum_tensor(f"{name}_pt", [P, 8, 512], fp32))
        stated, aggregated, eps_set, rooted, inverted, normed, turned, even_out, odd_out = sems(
            nc, k, name, "stated aggregated eps_set rooted inverted normed turned even_out odd_out")
        with nc.Block() as block:

            @block.gpsimd
            def _(pool):
                nc.gpsimd.memset(eps[:, :], EPS).then_inc(eps_set, 1)

            @block.scalar
            def _(act):
                act.wait_ge(eps_set, 1)
                act.wait_ge(aggregated, NT)
                nc.scalar.activation(std[:, :], mv[:, :, 1], ACT.Sqrt, bias=eps[:, 0:1]).then_inc(rooted, 1)
                for t in range(0, NT, 2):
                    act.wait_ge(turned, t + 1)
                    nc.scalar.activation(xT[:, :, t * P:(t + 1) * P],
                                         pt[:, t % 8, 0:D].rearrange("p (c n) -> p c n", c=DC),
                                         ACT.Copy).then_inc(even_out, 1)

            @block.vector
            def _(dve):
                for t in range(NT):
                    nc.vector.bn_stats(stats[:, t, :], h[:, t, :]).then_inc(stated, 1)
                for t in range(NT):
                    dve.wait_ge(stated, t + 1)
                    nc.vector.bn_aggr(mv[:, t, :], stats[:, t, :]).then_inc(aggregated, 1)
                dve.wait_ge(rooted, 1)
                nc.vector.reciprocal(rstd[:, :], std[:, :]).then_inc(inverted, 1)
                dve.wait_ge(aggregated, NT)
                dve.wait_ge(inverted, 1)

                def move(t):
                    dve.wait_ge(turned, t + 1)
                    nc.vector.tensor_copy(xT[:, :, t * P:(t + 1) * P],
                                          pt[:, t % 8, 0:D].rearrange("p (c n) -> p c n", c=DC)).then_inc(odd_out, 1)

                for t in range(NT):
                    nc.vector.tensor_scalar(xn[:, t, :], h[:, t, :], mv[:, t, 0:1], rstd[:, t:t + 1],
                                            ALU.subtract, ALU.mult).then_inc(normed, 1)
                    if t % 2 and t >= 3:
                        move(t - 2)
                move(NT - 2)

            @block.tensor
            def _(pe):
                for t in range(NT):
                    pe.wait_ge(normed, t + 1)
                    if t >= 8:
                        pe.wait_ge(odd_out if t % 2 else even_out, (t - 8) // 2 + 1)
                    for c in range(DC):
                        mm = nc.tensor.transpose(pt[:, t % 8, c * P:(c + 1) * P],
                                                 xn[:, t, c * P:(c + 1) * P], ident)
                    mm.then_inc(turned, 1)


def store(nc, k, out):
    h = k["h"]
    with ExitStack() as st:
        (stored,) = sems(nc, k, "store", "stored")
        with nc.Block() as block:

            @block.sync
            def _(sp):
                sp.dma_start(out.rearrange("(t p) d -> p t d", p=P), h[:, :, :]).then_inc(stored, 16)
                sp.wait_ge(stored, 16)


def window_attention(nc, a, k):
    h, xT = k["h"], k["xT"]
    ident = k["const"]("ident")
    NBLK = B // ABLK
    CB = ABLK * S
    VW = HD + 1
    with ExitStack() as st:
        sb = lambda n, s, d=fp32: k["sb"](f"wa_{n}", s, d, st)
        wq, wk, wv, wo = (sb(n, [P, DC, D]) for n in ("wq", "wk", "wv", "wo"))
        bq, bk, bv = (sb(n, [P, DC]) for n in ("bq", "bk", "bv"))
        bo = sb("bo", [P, D])
        xb = sb("xb", [P, DC, CB])
        qT = sb("qT", [P, DC, CB])
        kT = sb("kT", [P, DC, CB])
        kheads = sb("kheads", [P, 2, HC, S])
        vals = sb("vals", [S, ABLK, H, VW])
        probs = sb("probs", [S, 4, HC, S])
        probsT = sb("probsT", [S, 2, HC, S])
        peak = sb("peak", [S, 2, HC])
        invsum = sb("invsum", [S, 2, HC])
        outs = sb("outs", [S, 2, P])
        aT = sb("aT", [P, DC, T])
        mask = sb("mask", [S, HC // 2, S], bf16)
        ident_b = sb("ident_b", [S, S], bf16)
        s_attn = st.enter_context(ExitStack())
        pscore = s_attn.enter_context(nc.psum_tensor("wa_scores", [P, 2, 2, 512], fp32))
        pturn = s_attn.enter_context(nc.psum_tensor("wa_turn", [P, 2, 512], fp32))
        pout = s_attn.enter_context(nc.psum_tensor("wa_out", [P, 512], fp32))
        pjob = s_attn.enter_context(nc.psum_tensor("wa_job", [P, 512], fp32))
        (w_in, block_copied, keys_spread, mask_set, ones_set, scored, turned, weighted, jobs_done, jobs_moved,
         peaked, shifted, exped, turn_moved, inverted, normalised, biased) = sems(
            nc, k, "wa", "w_in block_copied keys_spread mask_set ones_set scored turned weighted jobs_done "
            "jobs_moved peaked shifted exped turn_moved inverted normalised biased")

        def four(ap):
            return ap.rearrange("q (g m) n -> q g m n", g=2)

        def jobs(step, first, last):
            before = ("v", step) if step < ABLK else None
            behind = (("q1", "k1")[step], 1) if step < 2 else (("q0", "k0")[step - 4], 0) if step in (4, 5) and not last else None
            late = None if first and step < 4 else ("out", step)
            return [before, behind, late]

        def numbered(first, last):
            n, table = 0, []
            for step in range(UNITS):
                table.append([])
                for job in jobs(step, first, last):
                    table[-1].append(job and (n, job))
                    n += job is not None
            return table, n

        def number(table, name):
            return next(job[0] for row in table for job in row if job and job[1][0] == name)

        def last_value(table):
            return table[ABLK - 1][0][0]

        first_jobs, n_first = numbered(True, False)
        mid_jobs, n_mid = numbered(False, False)
        last_jobs, n_last = numbered(False, True)
        PRO = 2

        def job_count(blk, n):
            return PRO + n if isinstance(blk, int) and blk == 0 else PRO + n_first + (blk - 1) * n_mid + n

        def blocks(eng, body):
            body(0, first_jobs)
            with eng.Fori(1, NBLK - 1, 1) as blk:
                body(blk, mid_jobs)
            body(NBLK - 1, last_jobs)

        with nc.Block() as block:

            @block.sync
            def _(sp):
                for dst, src in ((wq, "wq"), (wk, "wk"), (wv, "wv"), (wo, "wo")):
                    sp.dma_start(dst[:, :, :], a[src]).then_inc(w_in, 16)
                for dst, src in ((bq, "bq"), (bk, "bk"), (bv, "bv")):
                    sp.dma_start(dst[:, :], a[src]).then_inc(w_in, 16)
                sp.dma_start(bo[:, :], a["bo"].broadcast_to([P, D])).then_inc(w_in, 16)

            @block.gpsimd
            def _(pool):
                nc.gpsimd.tensor_copy(xb[:, :, :], xT[:, :, 0:CB]).then_inc(block_copied, 1)
                nc.gpsimd.tensor_copy(ident_b[:, :], ident[0:S, 0:S]).then_inc(mask_set, 1)
                nc.gpsimd.tensor_copy(mask[:, :, :], k["const"]("mask").unsqueeze(1).broadcast_to([S, HC // 2, S]))\
                    .then_inc(mask_set, 1)
                nc.gpsimd.memset(vals[:, :, :, HD:VW], 1.0).then_inc(ones_set, 1)
                head_of = k["const"]("head_of").unsqueeze(2).broadcast_to([P, HC, S])
                pool.wait_ge(w_in, 128)
                for t in range(NT):
                    nc.gpsimd.tensor_tensor(h[:, t, :], h[:, t, :], bo[:, :], ALU.add).then_inc(biased, 1)

                def body(blk, table):
                    for step in range(UNITS):
                        c, b = step // ABLK, step % ABLK
                        if c == 0:
                            if isinstance(blk, int) and blk == 0:
                                pool.wait_ge(jobs_moved, PRO)
                            else:
                                pool.wait_ge(jobs_moved, job_count(blk, 0))
                        else:
                            pool.wait_ge(jobs_moved, job_count(blk, number(table, "k1") + 1))
                        if not (isinstance(blk, int) and blk == 0 and step < 2):
                            pool.wait_ge(scored, blk * UNITS + step - 1)
                        nc.gpsimd.tensor_tensor(
                            kheads[:, step % 2, :, :],
                            kT[:, c, b * S:(b + 1) * S].unsqueeze(1).broadcast_to([P, HC, S]),
                            head_of, ALU.mult).then_inc(keys_spread, 1)
                        if step == 5 and table is not last_jobs:
                            pool.wait_ge(jobs_done, job_count(blk, last_value(table) + 1))
                            nc.gpsimd.tensor_copy(xb[:, :, :], xT[:, :, bass.ds((blk + 1) * CB, CB)])\
                                .then_inc(block_copied, 1)

                blocks(pool, body)

            @block.tensor
            def _(pe):
                def project(w, m, cols):
                    for c in range(DC):
                        mm = nc.tensor.matmul(pjob[:, 0:CB], w[:, c, m * P:(m + 1) * P], cols(c),
                                              start=(c == 0), stop=(c == DC - 1))
                    mm.then_inc(jobs_done, 1)

                pe.wait_ge(w_in, 128)
                project(wq, 0, lambda c: xT[:, c, 0:CB])
                pe.wait_ge(jobs_moved, 1)
                project(wk, 0, lambda c: xT[:, c, 0:CB])
                pe.wait_ge(mask_set, 2)

                def do_job(blk, n, job):
                    kind, which = job
                    pe.wait_ge(jobs_moved, job_count(blk, n))
                    if kind == "out":
                        unit = blk * UNITS + which - 4
                        pe.wait_ge(normalised, unit + 1)
                        nc.tensor.transpose(pjob[:, 0:S], outs[:, which % 2, :], ident[0:S, 0:S]).then_inc(jobs_done, 1)
                    elif kind == "v":
                        if which == 0:
                            pe.wait_ge(block_copied, blk + 1)
                        for c in range(DC):
                            mm = nc.tensor.matmul(pjob[0:S, 0:D], xb[:, c, which * S:(which + 1) * S], wv[:, c, :],
                                                  start=(c == 0), stop=(c == DC - 1))
                        mm.then_inc(jobs_done, 1)
                    else:
                        ahead = 0 if which else 1
                        project(wq if kind[0] == "q" else wk, which,
                                lambda c: xT[:, c, bass.ds((blk + ahead) * CB, CB)])

                def turn(unit, slot4, slot2, first):
                    pe.wait_ge(exped, unit + 1)
                    if not first:
                        pe.wait_ge(turn_moved, unit)
                    for hd in range(HC):
                        mm = nc.tensor.transpose(pturn[0:S, hd // 4, (hd % 4) * S:(hd % 4 + 1) * S],
                                                 probs[:, slot4, hd, :], ident[0:S, 0:S])
                    mm.then_inc(turned, 1)

                def weigh(unit, slot2, img, c, first):
                    pe.wait_ge(turn_moved, unit + 1)
                    if not first:
                        pe.wait_ge(normalised, unit)
                    for hd in range(HC):
                        mm = nc.tensor.matmul(pout[0:S, hd * VW:(hd + 1) * VW], probsT[:, slot2, hd, :],
                                              vals[:, img, c * HC + hd, :], start=True, stop=True)
                    mm.then_inc(weighted, 1)

                def body(blk, table):
                    start = isinstance(blk, int) and blk == 0
                    for step in range(UNITS):
                        c, b = step // ABLK, step % ABLK
                        before, behind, late = table[step]
                        if before:
                            do_job(blk, *before)
                        pe.wait_ge(keys_spread, blk * UNITS + step + 1)
                        if not (start and step < 2):
                            pe.wait_ge(shifted, blk * UNITS + step - 1)
                        if step == 4:
                            pe.wait_ge(jobs_moved, job_count(blk, number(table, "k1") + 1))
                        for g in range(2):
                            bank = pscore[0:S, step % 2, g, 0:4 * S]
                            nc.tensor.matmul(bank, ident_b[:, :], mask[:, :, :].rearrange("q m n -> q (m n)"),
                                             start=True, stop=False)
                            mm = nc.tensor.matmul(bank, qT[:, c, b * S:(b + 1) * S],
                                                  kheads[:, step % 2, 4 * g:4 * g + 4, :].rearrange("p m n -> p (m n)"),
                                                  start=False, stop=True)
                        mm.then_inc(scored, 1)
                        if behind:
                            do_job(blk, *behind)
                        unit = blk * UNITS + step
                        if not (start and step < 2):
                            turn(unit - 2, (step - 2) % 4, step % 2, start and step == 2)
                        if late:
                            do_job(blk, *late)
                        if not (start and step < 3):
                            v = (step - 3) % UNITS
                            weigh(unit - 3, (step - 3) % 2, v % ABLK, v // ABLK, start and step == 3)

                blocks(pe, body)
                n_units = NBLK * UNITS
                done = job_count(NBLK - 1, n_last)
                for step in range(4):
                    pe.wait_ge(jobs_moved, done + step)
                    pe.wait_ge(normalised, n_units + step - 3)
                    nc.tensor.transpose(pjob[:, 0:S], outs[:, step % 2, :], ident[0:S, 0:S]).then_inc(jobs_done, 1)
                    if step < 2:
                        turn(n_units + step - 2, (step - 2) % 4, step % 2, False)
                    if step < 3:
                        v = (step - 3) % UNITS
                        weigh(n_units + step - 3, (step - 3) % 2, v % ABLK, v // ABLK, False)

            @block.vector
            def _(dve):
                def normalise(unit, slot):
                    dve.wait_ge(weighted, unit + 1)
                    out3 = pout[0:S, 0:HC * VW].rearrange("q (m v) -> q m v", v=VW)
                    nc.vector.reciprocal(invsum[:, slot, :], out3[:, :, HD]).then_inc(inverted, 1)
                    dve.wait_ge(inverted, unit + 1)
                    nc.vector.tensor_tensor(outs[:, slot, :].rearrange("q (m v) -> q m v", v=HD), out3[:, :, 0:HD],
                                            invsum[:, slot, :].unsqueeze(2).broadcast_to([S, HC, HD]),
                                            ALU.mult).then_inc(normalised, 1)

                def body(blk, table):
                    start = isinstance(blk, int) and blk == 0
                    for step in range(UNITS):
                        unit = blk * UNITS + step
                        scores = pscore[0:S, step % 2, :, 0:4 * S].rearrange("q g (m n) -> q g m n", n=S)
                        dve.wait_ge(scored, unit + 1)
                        nc.vector.tensor_reduce(peak[:, step % 2, :], scores, AX.X, ALU.max).then_inc(peaked, 1)
                        dve.wait_ge(peaked, unit + 1)
                        if not (start and step < 4):
                            dve.wait_ge(turned, unit - 3)
                        peaks = peak[:, step % 2, :].rearrange("q (g m) -> q g m", g=2)
                        nc.vector.tensor_tensor(four(probs[:, step % 4, :, :]), scores,
                                                peaks.unsqueeze(3).broadcast_to([S, 2, HC // 2, S]),
                                                ALU.subtract).then_inc(shifted, 1)
                        if not (start and step < 3):
                            normalise(unit - 3, (step - 3) % 2)

                blocks(dve, body)
                for step in range(3):
                    normalise(NBLK * UNITS + step - 3, (step - 3) % 2)

            @block.scalar
            def _(act):
                scale = float(HD) ** -0.5

                def move_job(blk, n, job):
                    kind, which = job
                    act.wait_ge(jobs_done, job_count(blk, n + 1))
                    if kind == "out":
                        place_out(blk, which)
                    elif kind == "v":
                        nc.scalar.activation(vals[:, which, :, 0:HD],
                                             pjob[0:S, 0:D].rearrange("s (m v) -> s m v", v=HD),
                                             ACT.Copy).then_inc(jobs_moved, 1)
                    else:
                        dst, bias = (qT, bq) if kind[0] == "q" else (kT, bk)
                        nc.scalar.activation(dst[:, which, :], pjob[:, 0:CB], ACT.Identity,
                                             bias=bias[:, which:which + 1]).then_inc(jobs_moved, 1)

                def place_out(blk, step):
                    back = (step - 4) % UNITS
                    c, b = back // ABLK, back % ABLK
                    at_blk = blk if step >= 4 else blk - 1
                    nc.scalar.activation(aT[:, c, bass.ds(at_blk * CB + b * S, S)], pjob[:, 0:S], ACT.Identity,
                                         bias=bv[:, c:c + 1]).then_inc(jobs_moved, 1)

                def exp(unit, slot):
                    act.wait_ge(shifted, unit + 1)
                    nc.scalar.activation(probs[:, slot, :, :], probs[:, slot, :, :], ACT.Exp, scale=scale)\
                        .then_inc(exped, 1)

                def move_turned(unit, slot):
                    act.wait_ge(turned, unit + 1)
                    nc.scalar.activation(four(probsT[:, slot, :, :]),
                                         pturn[0:S, :, 0:4 * S].rearrange("q g (m n) -> q g m n", n=S),
                                         ACT.Copy).then_inc(turn_moved, 1)

                act.wait_ge(w_in, 128)
                act.wait_ge(ones_set, 1)
                act.wait_ge(jobs_done, 1)
                nc.scalar.activation(qT[:, 0, :], pjob[:, 0:CB], ACT.Identity, bias=bq[:, 0:1]).then_inc(jobs_moved, 1)
                act.wait_ge(jobs_done, 2)
                nc.scalar.activation(kT[:, 0, :], pjob[:, 0:CB], ACT.Identity, bias=bk[:, 0:1]).then_inc(jobs_moved, 1)

                def body(blk, table):
                    start = isinstance(blk, int) and blk == 0
                    for step in range(UNITS):
                        unit = blk * UNITS + step
                        before, behind, late = table[step]
                        if before:
                            move_job(blk, *before)
                        if not (start and step < 1):
                            exp(unit - 1, (step - 1) % 4)
                        if behind:
                            move_job(blk, *behind)
                        if not (start and step < 2):
                            move_turned(unit - 2, step % 2)
                        if late:
                            move_job(blk, *late)

                blocks(act, body)
                n_units = NBLK * UNITS
                done = job_count(NBLK - 1, n_last)
                for step in range(4):
                    act.wait_ge(jobs_done, done + step + 1)
                    place_out(NBLK, step)
                    if step < 1:
                        exp(n_units - 1, 3)
                    if step < 2:
                        move_turned(n_units + step - 2, step % 2)

        s_attn.close()
        project_out(nc, k, st, "wo", aT, wo)


def project_out(nc, k, st, name, aT, w):
    h = k["h"]
    ps = st.enter_context(nc.psum_tensor(f"{name}_ps", [P, 8, 512], fp32))
    projected, added = sems(nc, k, name, "projected added")
    with nc.Block() as block:

        @block.tensor
        def _(pe):
            for t in range(NT):
                if t >= 8:
                    pe.wait_ge(added, t - 7)
                for c in range(DC):
                    mm = nc.tensor.matmul(ps[:, t % 8, 0:D], aT[:, c, t * P:(t + 1) * P], w[:, c, :],
                                          start=(c == 0), stop=(c == DC - 1))
                mm.then_inc(projected, 1)

        @block.vector
        def _(dve):
            for t in range(NT):
                dve.wait_ge(projected, t + 1)
                nc.vector.tensor_tensor(h[:, t, :], h[:, t, :], ps[:, t % 8, 0:D], ALU.add).then_inc(added, 1)


def places(k, st, name, E, K, n_slots):
    sb = lambda n, s, d=fp32: k["sb"](f"{name}_{n}", s, d, st)
    return dict(
        E=E, K=K, n_slots=n_slots,
        chosen=sb("chosen", [P, NT, E]),
        chosen_b=sb("chosen_b", [P, NT, E], bf16),
        before_b=sb("before_b", [P, P], bf16),
        ones_b=sb("ones_b", [P, P], bf16),
        iota_h=sb("iota_h", [P, SLOTS0], fp16),
        rank=sb("rank", [P, NT, E]),
        off=sb("off", [P, NT + 1, E]),
        tiles=sb("tiles", [P, E]), tiles_i=sb("tiles_i", [P, E], i32),
        zeros=sb("zeros", [P, E]), ends=sb("ends", [P, E]), base=sb("base", [P, E]),
        slot8=sb("slot8", [P, NT, 8]),
        slot=sb("slot", [P, NT, K]), slot_i=sb("slot_i", [P, NT, K], i32),
        hi_i=sb("hi_i", [P, NT, K], i32), lo_i=sb("lo_i", [P, NT, K], i32),
        hi=sb("hi", [P, NT, K]), lo=sb("lo", [P, NT, K]),
        lo_hot=sb("lo_hot", [P, 8, P], fp16), hi_hot=sb("hi_hot", [P, 8, n_slots], fp16),
        below=sb("below", [P, E]), tile_expert=sb("tile_expert", [P, 2]), tile_expert_i=sb("tile_expert_i", [P, 2], i32),
    )


def count_places(nc, dve, link, r, pcount, ranks_ready, totals_ready, ranks_out):
    E, K = r["E"], r["K"]
    dve.wait_ge(ranks_ready, 1)
    for t0, n, ap in banks(pcount, E):
        last = nc.vector.tensor_copy(r["rank"][:, t0:t0 + n, :], ap)
    link(last)
    last_out = nc.vector.memset(r["off"][:, 0, :], 0.0)
    last_out.then_inc(ranks_out, 1)
    dve.wait_ge(totals_ready, 1)
    link(nc.vector.memset(r["zeros"][:, :], 0.0))
    for t0, n, ap in banks(pcount, E):
        for t in range(t0, t0 + n):
            link(nc.vector.tensor_tensor(r["off"][:, t + 1, :], r["off"][:, t, :], ap[:, t - t0, :], ALU.add))
    link(nc.vector.tensor_scalar(r["tiles_i"][:, :], r["off"][:, NT, :], float(P - 1), None, ALU.add))
    link(nc.vector.tensor_scalar(r["tiles_i"][:, :], r["tiles_i"][:, :], 7, None, ALU.arith_shift_right))
    link(nc.vector.tensor_copy(r["tiles"][:, :], r["tiles_i"][:, :]))
    link(nc.vector.tensor_tensor_scan(r["ends"][:, :], r["tiles"][:, :], r["zeros"][:, :], 0.0, ALU.add, ALU.add))
    link(nc.vector.tensor_tensor(r["base"][:, :], r["ends"][:, :], r["tiles"][:, :], ALU.subtract))
    link(nc.vector.tensor_scalar(r["base"][:, :], r["base"][:, :], float(P), 1.0, ALU.mult, ALU.add))
    link(nc.vector.tensor_tensor(r["rank"][:, :, :], r["rank"][:, :, :], r["off"][:, 0:NT, :], ALU.add))
    link(nc.vector.tensor_tensor(r["rank"][:, :, :], r["rank"][:, :, :],
                                 r["base"][:, :].unsqueeze(1).broadcast_to([P, NT, E]), ALU.add))
    link(nc.vector.tensor_tensor(r["rank"][:, :, :], r["rank"][:, :, :], r["chosen"][:, :, :], ALU.mult))
    for t in range(NT):
        last = nc.vector.max(r["slot8"][:, t, :], r["rank"][:, t, :])
    link(last)
    link(nc.vector.tensor_scalar(r["slot"][:, :, :], r["slot8"][:, :, 0:K], 1.0, None, ALU.subtract))
    link(nc.vector.tensor_copy(r["slot_i"][:, :, :], r["slot"][:, :, :]))
    link(nc.vector.tensor_scalar(r["hi_i"][:, :, :], r["slot_i"][:, :, :], 7, None, ALU.arith_shift_right))
    link(nc.vector.tensor_scalar(r["lo_i"][:, :, :], r["slot_i"][:, :, :], P - 1, None, ALU.bitwise_and))
    link(nc.vector.tensor_copy(r["hi"][:, :, :], r["hi_i"][:, :, :]))
    link(nc.vector.tensor_copy(r["lo"][:, :, :], r["lo_i"][:, :, :]))


def tile_experts(nc, k, link, r, written):
    E = r["E"]
    for q in range(2):
        link(nc.vector.tensor_scalar(r["below"][:, :], r["ends"][:, :], k["const"]("slot_tile")[:, q:q + 1], None,
                                     ALU.is_le, ALU.add, accum_out=r["tile_expert"][:, q:q + 1]))
    link(nc.vector.tensor_scalar(r["tile_expert"][:, :], r["tile_expert"][:, :], float(E - 1), None, ALU.min))
    nc.vector.tensor_copy(r["tile_expert_i"][:, :], r["tile_expert"][:, :]).then_inc(written, 1)


def banks(ps, E):
    per = 512 // E
    for t0 in range(0, NT, per):
        n = min(per, NT - t0)
        b = t0 // per
        yield t0, n, ps[:, b, 0:n * E].rearrange("p (t e) -> p t e", e=E)


def hot_pair(nc, k, r, t, kk, slot):
    iota, token = r["iota_h"], k["const"]("token")
    lo, hi = r["lo"], r["hi"]
    if isinstance(t, int):
        lo1, hi1, tk = lo[:, t, kk:kk + 1], hi[:, t, kk:kk + 1], token[:, t:t + 1]
    else:
        lo1, hi1 = lo[:, bass.ds(t, 1), kk], hi[:, bass.ds(t, 1), kk]
        tk = token[:, bass.ds(t, 1)]
    nc.vector.tensor_scalar(r["lo_hot"][:, slot, :], iota[:, 0:P], lo1, None, ALU.is_equal)
    return nc.vector.tensor_scalar(r["hi_hot"][:, slot, :], iota[:, 0:r["n_slots"]], hi1, tk, ALU.is_equal, ALU.mult)


def mixture_0(nc, a, k):
    h, xn, xT = k["h"], k["xn"], k["xT"]
    ident = k["const"]("ident")
    RE = NT * E0
    with ExitStack() as st:
        sb = lambda n, s, d=fp32: k["sb"](f"m0_{n}", s, d, st)
        x_rows = nc.dram_tensor("m0_x_rows", (T, D), fp32).ap()
        y_rows = nc.dram_tensor("m0_y_rows", (SLOTS0 * P, D), fp32).ap()
        experts_dram = nc.dram_tensor("m0_tile_experts", (2, P), i32).ap()
        coef = sb("coef", [P, NT, E0])
        ids = sb("ids", [P, SLOTS0], u32)
        tile_expert_row = sb("tile_expert_row", [1, 2 * P], i32)
        r = places(k, st, "m0", E0, K0, SLOTS0)

        with ExitStack() as rs:
            rb = lambda n, s, d=fp32: k["sb"](f"m0_{n}", s, d, rs)
            router = rb("router", [P, DC, E0])
            e_bias = rb("e_bias", [P, E0])
            up = rb("shared_up", [P, DC, 2 * D])
            down = rb("shared_down", [P, DC, D])
            score = rb("score", [P, NT, E0])
            biased = rb("biased", [P, NT, E0])
            top1, low1 = rb("top1", [P, NT * G0, 4]), rb("low1", [P, NT * G0, 4])
            top2, low2, mid2 = (rb(n, [P, NT * G0, 2]) for n in ("top2", "low2", "mid2"))
            top3, low3, mid3 = (rb(n, [P, NT * G0]) for n in ("top3", "low3", "mid3"))
            group = rb("group", [P, NT, G0])
            above, level = (rb(n, [P, NT, G0 * G0]) for n in ("above", "level"))
            kept = rb("kept", [P, NT * G0])
            best8 = rb("best8", [P, NT, 8])
            wsum = rb("wsum", [P, NT])
            gate_act = rb("gate_act", [P, 2, D])
            up_sb = rb("up_sb", [P, 2, D])
            hid = rb("hid", [P, 2, D])
            down_sb = rb("down_sb", [P, 2, D])
            pcount = rs.enter_context(nc.psum_tensor("m0_pcount", [P, 3, 512], fp32))
            ptable = rs.enter_context(nc.psum_tensor("m0_ptable", [P, 512], fp32))
            pup = rs.enter_context(nc.psum_tensor("m0_pup", [P, 2, 512], fp32))
            pdown = rs.enter_context(nc.psum_tensor("m0_pdown", [P, 2, 512], fp32))
            (w_in, rows_out, logits, scored, chain, chosen_ready, set_up, ranks, ranks_out, totals, hot, hot_used,
             tabled, experts_ready, experts_out, experts_back, up_done, gated, up_moved, hid_ready, down_done,
             down_moved, shared_added) = sems(
                nc, k, "m0r", "w_in rows_out logits scored chain chosen_ready set_up ranks ranks_out totals hot "
                "hot_used tabled experts_ready experts_out experts_back up_done gated up_moved hid_ready down_done "
                "down_moved shared_added")
            with nc.Block() as block:

                @block.sync
                def _(sp):
                    sp.dma_start(router[:, :, :], a["router"]).then_inc(w_in, 16)
                    sp.dma_start(e_bias[:, :], a["e_bias"].broadcast_to([P, E0])).then_inc(w_in, 16)
                    sp.dma_start(up[:, :, :], a["shared_up"]).then_inc(w_in, 16)
                    sp.dma_start(down[:, :, :], a["shared_down"]).then_inc(w_in, 16)
                    sp.dma_start(x_rows.rearrange("(t p) d -> p t d", p=P), xn[:, :, :]).then_inc(rows_out, 16)
                    sp.wait_ge(experts_ready, 1)
                    sp.dma_start(experts_dram.rearrange("q p -> p q"), r["tile_expert_i"][:, :],
                                 allow_slow_non_contiguous=True).then_inc(experts_out, 16)
                    sp.wait_ge(experts_out, 16)
                    sp.dma_start(tile_expert_row[:, :], experts_dram.rearrange("(o q) p -> o (q p)", o=1))\
                        .then_inc(experts_back, 16)
                    sp.wait_ge(experts_back, 16)
                    sp.wait_ge(rows_out, 16)

                @block.gpsimd
                def _(pool):
                    nc.gpsimd.tensor_copy(r["before_b"][:, :], k["const"]("before")).then_inc(set_up, 1)
                    nc.gpsimd.memset(r["ones_b"][:, :], 1.0).then_inc(set_up, 1)
                    nc.gpsimd.tensor_copy(r["iota_h"][:, :], k["const"]("iota")).then_inc(set_up, 1)
                    for t in range(NT):
                        pool.wait_ge(up_moved, t + 1)
                        if t >= 2:
                            pool.wait_ge(down_done, t - 1)
                        nc.gpsimd.tensor_tensor(hid[:, t % 2, :], gate_act[:, t % 2, :], up_sb[:, t % 2, :],
                                                ALU.mult).then_inc(hid_ready, 1)
                        if t >= 1:
                            pool.wait_ge(down_moved, t)
                            nc.gpsimd.tensor_tensor(h[:, t - 1, :], h[:, t - 1, :], down_sb[:, (t - 1) % 2, :],
                                                    ALU.add).then_inc(shared_added, 1)
                    pool.wait_ge(down_moved, NT)
                    nc.gpsimd.tensor_tensor(h[:, NT - 1, :], h[:, NT - 1, :], down_sb[:, (NT - 1) % 2, :],
                                            ALU.add).then_inc(shared_added, 1)

                @block.scalar
                def _(act):
                    act.wait_ge(logits, 1)
                    for t0, n, ap in banks(pcount, E0):
                        last = nc.scalar.activation(score[:, t0:t0 + n, :], ap, ACT.Sigmoid)
                    last.then_inc(scored, 1)

                    def move_down(t):
                        act.wait_ge(down_done, t + 1)
                        if t >= 2:
                            act.wait_ge(shared_added, t - 1)
                        nc.scalar.activation(down_sb[:, t % 2, :], pdown[:, t % 2, 0:D], ACT.Copy).then_inc(down_moved, 1)

                    for t in range(NT):
                        act.wait_ge(up_done, t + 1)
                        if t >= 2:
                            act.wait_ge(hid_ready, t - 1)
                        nc.scalar.activation(gate_act[:, t % 2, :], pup[:, t % 2, 0:D], ACT.Silu)
                        nc.scalar.activation(up_sb[:, t % 2, :], pup[:, t % 2, D:2 * D], ACT.Copy).then_inc(up_moved, 1)
                        if t >= 1:
                            move_down(t - 1)
                    move_down(NT - 1)

                @block.tensor
                def _(pe):
                    pe.wait_ge(w_in, 64)
                    for t0, n, ap in banks(pcount, E0):
                        for t in range(t0, t0 + n):
                            for c in range(DC):
                                mm = nc.tensor.matmul(ap[:, t - t0, :], xT[:, c, t * P:(t + 1) * P], router[:, c, :],
                                                      start=(c == 0), stop=(c == DC - 1))
                    mm.then_inc(logits, 1)

                    def counts(lhsT):
                        for t0, n, _ in banks(pcount, E0):
                            mm = nc.tensor.matmul(pcount[:, t0 // 8, 0:n * E0], lhsT,
                                                  r["chosen_b"][:, t0:t0 + n, :].rearrange("p t e -> p (t e)"),
                                                  start=True, stop=True)
                        return mm

                    def shared_down(t):
                        pe.wait_ge(hid_ready, t + 1)
                        if t >= 2:
                            pe.wait_ge(down_moved, t - 1)
                        for c in range(DC):
                            mm = nc.tensor.matmul(pdown[:, t % 2, 0:D], hid[:, t % 2, c * P:(c + 1) * P], down[:, c, :],
                                                  start=(c == 0), stop=(c == DC - 1))
                        mm.then_inc(down_done, 1)

                    for t in range(NT):
                        if t >= 2:
                            pe.wait_ge(up_moved, t - 1)
                        for m in range(4):
                            for c in range(DC):
                                mm = nc.tensor.matmul(pup[:, t % 2, m * P:(m + 1) * P], up[:, c, m * P:(m + 1) * P],
                                                      xT[:, c, t * P:(t + 1) * P], start=(c == 0), stop=(c == DC - 1))
                        mm.then_inc(up_done, 1)
                        if t >= 1:
                            shared_down(t - 1)
                        if t == 12:
                            pe.wait_ge(set_up, 3)
                            pe.wait_ge(chosen_ready, 1)
                            counts(r["before_b"][:, :]).then_inc(ranks, 1)
                        if t == 13:
                            pe.wait_ge(ranks_out, 1)
                            counts(r["ones_b"][:, :]).then_inc(totals, 1)
                    shared_down(NT - 1)
                    gather_table(nc, pe, r, ptable, hot, hot_used, tabled)

                @block.vector
                def _(dve):
                    done = [0]

                    def link(ins):
                        done[0] += 1
                        ins.then_inc(chain, 1)
                        dve.wait_ge(chain, done[0])

                    vt = nc.vector.tensor_tensor
                    dve.wait_ge(w_in, 64)
                    dve.wait_ge(scored, 1)
                    link(vt(biased[:, :, :], score[:, :, :], e_bias[:, :].unsqueeze(1).broadcast_to([P, NT, E0]), ALU.add))
                    b8 = biased[:, :, :].rearrange("p t (g e) -> p (t g) e", g=G0)
                    vt(top1[:, :, :], b8[:, :, 0:4], b8[:, :, 4:8], ALU.max)
                    link(vt(low1[:, :, :], b8[:, :, 0:4], b8[:, :, 4:8], ALU.min))
                    vt(top2[:, :, :], top1[:, :, 0:2], top1[:, :, 2:4], ALU.max)
                    vt(mid2[:, :, :], top1[:, :, 0:2], top1[:, :, 2:4], ALU.min)
                    link(vt(low2[:, :, :], low1[:, :, 0:2], low1[:, :, 2:4], ALU.max))
                    link(vt(low2[:, :, :], low2[:, :, :], mid2[:, :, :], ALU.max))
                    vt(top3[:, :], top2[:, :, 0], top2[:, :, 1], ALU.max)
                    vt(mid3[:, :], top2[:, :, 0], top2[:, :, 1], ALU.min)
                    link(vt(low3[:, :], low2[:, :, 0], low2[:, :, 1], ALU.max))
                    link(vt(low3[:, :], low3[:, :], mid3[:, :], ALU.max))
                    link(vt(group[:, :, :].rearrange("p t g -> p (t g)"), top3[:, :], low3[:, :], ALU.add))
                    g_in = group[:, :, :].unsqueeze(3).broadcast_to([P, NT, G0, G0])
                    g_other = group[:, :, :].unsqueeze(2).broadcast_to([P, NT, G0, G0])
                    four = lambda x: x[:, :, :].rearrange("p t (g o) -> p t g o", g=G0)
                    vt(four(above), g_other, g_in, ALU.is_gt)
                    link(vt(four(level), g_other, g_in, ALU.is_equal))
                    link(vt(level[:, :, :], level[:, :, :],
                            k["const"]("group_before").unsqueeze(1).broadcast_to([P, NT, G0 * G0]), ALU.mult))
                    link(vt(above[:, :, :], above[:, :, :], level[:, :, :], ALU.add))
                    link(nc.vector.tensor_reduce(kept[:, :], above[:, :, :].rearrange("p t (g o) -> p (t g) o", g=G0),
                                                 AX.X, ALU.add))
                    link(nc.vector.tensor_scalar(kept[:, :], kept[:, :], float(KG), None, ALU.is_lt))
                    link(vt(b8, b8, kept[:, :].unsqueeze(2).broadcast_to([P, NT * G0, E0 // G0]), ALU.mult))
                    for t in range(NT):
                        last = nc.vector.max(best8[:, t, :], biased[:, t, :])
                    link(last)
                    for t in range(NT):
                        last = nc.vector.match_replace(r["rank"][:, t, :], best8[:, t, :], biased[:, t, :], REPLACED)
                    link(last)
                    nc.vector.tensor_scalar(r["chosen_b"][:, :, :], r["rank"][:, :, :], REPLACED, None, ALU.is_equal)\
                        .then_inc(chosen_ready, 1)
                    link(nc.vector.tensor_scalar(r["chosen"][:, :, :], r["rank"][:, :, :], REPLACED, None, ALU.is_equal))
                    link(vt(coef[:, :, :], score[:, :, :], r["chosen"][:, :, :], ALU.mult))
                    link(nc.vector.tensor_reduce(wsum[:, :], coef[:, :, :], AX.X, ALU.add))
                    link(nc.vector.tensor_scalar(wsum[:, :], wsum[:, :], 1e-20, None, ALU.add))
                    link(nc.vector.reciprocal(wsum[:, :], wsum[:, :]))
                    link(nc.vector.scalar_tensor_tensor(coef[:, :, :], coef[:, :, :], SCALE0,
                                                        wsum[:, :].unsqueeze(2).broadcast_to([P, NT, E0]),
                                                        ALU.mult, ALU.mult))
                    count_places(nc, dve, link, r, pcount, ranks, totals, ranks_out)
                    dve.wait_ge(set_up, 3)
                    one_hots(nc, dve, k, r, hot, hot_used)
                    tile_experts(nc, k, link, r, experts_ready)
                    dve.wait_ge(tabled, 1)
                    link(nc.vector.tensor_scalar(ids[:, :], ptable[:, 0:SLOTS0], float(TOK0), None, ALU.add))

        expert_tiles_0(nc, a, k, ids, tile_expert_row, x_rows, y_rows)
        combine_0(nc, k, r, coef, y_rows)


def one_hots(nc, dve, k, r, hot, hot_used):
    K = r["K"]
    per = 8 // K
    if K == 8:
        for kk in range(K):
            hot_pair(nc, k, r, 0, kk, kk).then_inc(hot, 1)
        with dve.Fori(1, NT, 1) as t:
            for kk in range(K):
                dve.wait_ge(hot_used, (t - 1) * K + kk + 1)
                hot_pair(nc, k, r, t, kk, kk).then_inc(hot, 1)
    else:
        for t in range(NT):
            if t >= per:
                dve.wait_ge(hot_used, t - per + 1)
            hot_pair(nc, k, r, t, 0, t % per).then_inc(hot, 1)


def gather_table(nc, pe, r, ptable, hot, hot_used, tabled):
    K, n = r["K"], r["n_slots"]

    def add(slot, start, stop):
        return nc.tensor.matmul(ptable[:, 0:n], r["lo_hot"][:, slot, :], r["hi_hot"][:, slot, :], start=start, stop=stop)

    if K == 8:
        for kk in range(K):
            pe.wait_ge(hot, kk + 1)
            add(kk, kk == 0, False).then_inc(hot_used, 1)
        with pe.Fori(1, NT - 1, 1) as t:
            for kk in range(K):
                pe.wait_ge(hot, t * K + kk + 1)
                add(kk, False, False).then_inc(hot_used, 1)
        for kk in range(K):
            pe.wait_ge(hot, (NT - 1) * K + kk + 1)
            mm = add(kk, False, kk == K - 1)
            mm.then_inc(tabled if kk == K - 1 else hot_used, 1)
    else:
        for t in range(NT):
            pe.wait_ge(hot, t + 1)
            mm = add(t % 8, t == 0, t == NT - 1)
            mm.then_inc(tabled if t == NT - 1 else hot_used, 1)


def expert_tiles_0(nc, a, k, ids, tile_expert_row, x_rows, y_rows):
    ident = k["const"]("ident")
    R = 8
    ROUNDS = SLOTS0 // R
    UNROLL = 4
    assert (ROUNDS - 1) % UNROLL == 0
    UP = DC * 2 * I0
    W = UP + D
    with ExitStack() as es:
        sb = lambda n, s, d=fp32: k["sb"](f"x0_{n}", s, d, es)
        w = sb("w", [P, R, W])
        idx = sb("idx", [P, R], u32)
        x = sb("x", [P, R, D])
        xt = sb("xt", [P, R, D])
        gate = sb("gate", [P, R, I0])
        hid = sb("hid", [P, R, I0])
        y = sb("y", [P, R, D])
        pturn = es.enter_context(nc.psum_tensor("x0_pturn", [P, 2, 512], fp32))
        pup = es.enter_context(nc.psum_tensor("x0_pup", [P, 2, 512], fp32))
        pdown = es.enter_context(nc.psum_tensor("x0_pdown", [P, 2, 512], fp32))
        (indexed, gathers, turned, turn_moved, up_done, gated, hid_ready, down_done, down_moved) = sems(
            nc, k, "x0", "indexed gathers turned turn_moved up_done gated hid_ready down_done down_moved")
        w_in = ring_sems(nc, k, "x0_w_in", R)
        x_in = ring_sems(nc, k, "x0_x_in", R)
        y_out = ring_sems(nc, k, "x0_y_out", R)
        with nc.Block() as block:

            def rounds(eng, body):
                body(True, 0)
                with eng.Fori(1, ROUNDS - UNROLL + 1, UNROLL) as n:
                    for u in range(UNROLL):
                        body(False, n + u)

            @block.sync
            def _(sp):
                def expert_of(n, s):
                    return sp.value_load(tile_expert_row[0:1, bass.ds(s * ROUNDS + n, 1)], min_val=0, max_val=E0 - 1)

                def rows_of(e):
                    return a["experts0"][bass.ds(e, 1), :, :].rearrange("o p n -> (o p) n")

                for s in range(R):
                    sp.dma_start(w[:, s, :], rows_of(expert_of(0, s))).then_inc(w_in[s], 16)
                with sp.Fori(1, ROUNDS - UNROLL + 1, UNROLL) as n:
                    for u in range(UNROLL):
                        for s in range(R):
                            e = expert_of(n + u, s)
                            sp.wait_ge(down_done, (n + u - 1) * R + s + 1)
                            sp.dma_start(w[:, s, :], rows_of(e)).then_inc(w_in[s], 16)

            @block.gpsimd
            def _(pool):
                def take_ids(n, s):
                    nc.gpsimd.tensor_copy(idx[:, s:s + 1], ids[:, bass.ds(s * ROUNDS + n, 1)]).then_inc(indexed, 1)

                def body(first, n):
                    for s in range(R):
                        ahead, at = (n, s + 1) if s + 1 < R else (n + 1, 0)
                        if not first or s + 1 == R:
                            pool.wait_ge(x_in[at], ahead * 16)
                        take_ids(ahead, at)
                        if not first:
                            pool.wait_ge(turned, (n - 1) * R + s + 1)
                        pool.wait_ge(indexed, n * R + s + 1)
                        pool.sem_inc(gathers, 1)
                        nc.gpsimd.indirect_dma_start(x[:, s, :], None, x_rows,
                                                     bass.IndirectOffsetOnAxis(ap=idx[:, s:s + 1], axis=0))\
                            .then_inc(x_in[s], 16)
                take_ids(0, 0)
                rounds(pool, body)

            @block.tensor
            def _(pe):
                def turn(first, n, s):
                    pe.wait_ge(x_in[s], (n + 1) * 16)
                    if not (first and s < 2):
                        pe.wait_ge(turn_moved, n * R + s - 1)
                    for c in range(DC):
                        mm = nc.tensor.transpose(pturn[:, s % 2, c * P:(c + 1) * P], x[:, s, c * P:(c + 1) * P], ident)
                    mm.then_inc(turned, 1)

                def up(j, s, rnd, early):
                    pe.wait_ge(w_in[s], (rnd + 1) * 16)
                    pe.wait_ge(turn_moved, j + 1)
                    if not early:
                        pe.wait_ge(hid_ready, j - 1)
                    for m in range(2):
                        for c in range(DC):
                            mm = nc.tensor.matmul(pup[:, s % 2, m * P:(m + 1) * P],
                                                  w[:, s, (m * DC + c) * I0:(m * DC + c + 1) * I0],
                                                  xt[:, s, c * P:(c + 1) * P], start=(c == 0), stop=(c == DC - 1))
                    mm.then_inc(up_done, 1)

                def down(j, s, early):
                    pe.wait_ge(hid_ready, j + 1)
                    if not early:
                        pe.wait_ge(down_moved, j - 1)
                    nc.tensor.matmul(pdown[:, s % 2, 0:D], hid[:, s, :], w[:, s, UP:W],
                                     start=True, stop=True).then_inc(down_done, 1)

                def body(first, n):
                    for s in range(R):
                        turn(first, n, s)
                        if not (first and s < 1):
                            up(n * R + s - 1, (s - 1) % R, n if s else n - 1, first and s < 3)
                        if not (first and s < 2):
                            down(n * R + s - 2, (s - 2) % R, first)

                rounds(pe, body)
                up(SLOTS0 - 1, R - 1, ROUNDS - 1, False)
                down(SLOTS0 - 2, R - 2, False)
                down(SLOTS0 - 1, R - 1, False)

            @block.scalar
            def _(act):
                def move_turned(first, j, s):
                    act.wait_ge(turned, j + 1)
                    if not first:
                        act.wait_ge(up_done, j - R + 1)
                    nc.scalar.activation(xt[:, s, :], pturn[:, s % 2, 0:D], ACT.Copy).then_inc(turn_moved, 1)

                def silu(early, j, s):
                    act.wait_ge(up_done, j + 1)
                    if not early:
                        act.wait_ge(hid_ready, j - R + 1)
                    nc.scalar.activation(gate[:, s, :], pup[:, s % 2, 0:P], ACT.Silu).then_inc(gated, 1)

                def store_y(n, s):
                    act.wait_ge(down_moved, n * R + s + 1)
                    act.dma_start(y_rows[bass.ds((s * ROUNDS + n) * P, P), :], y[:, s, :]).then_inc(y_out[s], 16)

                def body(first, n, second=False):
                    for s in range(R):
                        j = n * R + s
                        move_turned(first, j, s)
                        if not (first and s < 1):
                            silu(first or (second and s == 0), j - 1, (s - 1) % R)
                        if not (first and s < 3):
                            store_y(n if s >= 3 else n - 1, (s - 3) % R)

                body(True, 0)
                body(False, 1, True)
                for n in range(2, 1 + UNROLL):
                    body(False, n)
                with act.Fori(1 + UNROLL, ROUNDS - UNROLL + 1, UNROLL) as n:
                    for u in range(UNROLL):
                        body(False, n + u)
                silu(False, SLOTS0 - 1, R - 1)
                for j in range(SLOTS0 - 3, SLOTS0):
                    store_y(ROUNDS - 1, j % R)
                for s in range(R):
                    act.wait_ge(y_out[s], ROUNDS * 16)

            @block.vector
            def _(dve):
                def multiply(early, j, s):
                    dve.wait_ge(gated, j + 1)
                    if not early:
                        dve.wait_ge(down_done, j - R + 1)
                    nc.vector.tensor_tensor(hid[:, s, :], gate[:, s, :], pup[:, s % 2, P:2 * P], ALU.mult)\
                        .then_inc(hid_ready, 1)

                def move_down(early, j, s, rnd):
                    dve.wait_ge(down_done, j + 1)
                    if not early:
                        dve.wait_ge(y_out[s], rnd * 16)
                    nc.vector.tensor_copy(y[:, s, :], pdown[:, s % 2, 0:D]).then_inc(down_moved, 1)

                def body(first, n, second=False):
                    for s in range(R):
                        if not (first and s < 1):
                            multiply(first or (second and s == 0), n * R + s - 1, (s - 1) % R)
                        if not (first and s < 2):
                            move_down(first or (second and s < 2), n * R + s - 2, (s - 2) % R, n if s >= 2 else n - 1)

                body(True, 0)
                body(False, 1, True)
                for n in range(2, 1 + UNROLL):
                    body(False, n)
                with dve.Fori(1 + UNROLL, ROUNDS - UNROLL + 1, UNROLL) as n:
                    for u in range(UNROLL):
                        body(False, n + u)
                multiply(False, SLOTS0 - 1, R - 1)
                move_down(False, SLOTS0 - 2, R - 2, ROUNDS - 1)
                move_down(False, SLOTS0 - 1, R - 1, ROUNDS - 1)


def combine_0(nc, k, r, coef, y_rows):
    h = k["h"]
    with ExitStack() as cs:
        sb = lambda n, s, d=fp32: k["sb"](f"c0_{n}", s, d, cs)
        idx = sb("idx", [P, NT * K0], u32)
        y = sb("y", [P, 2, K0, D])
        wt = sb("wt", [P, NT, K0])
        picked = sb("picked", [P, E0])
        indexed, weighed, added = sems(nc, k, "c0", "indexed weighed added")
        y_in = ring_sems(nc, k, "c0_y_in", 2)
        with nc.Block() as block:

            @block.gpsimd
            def _(pool):
                nc.gpsimd.tensor_copy(idx[:, :], r["slot"][:, :, :].rearrange("p t k -> p (t k)")).then_inc(indexed, 1)
                pool.wait_ge(indexed, 1)
                for t in range(NT):
                    if t >= 2:
                        pool.wait_ge(added, (t - 1) * K0)
                    for kk in range(K0):
                        n = t * K0 + kk
                        nc.gpsimd.indirect_dma_start(y[:, t % 2, kk, :], None, y_rows,
                                                     bass.IndirectOffsetOnAxis(ap=idx[:, n:n + 1], axis=0))\
                            .then_inc(y_in[t % 2], 16)

            @block.vector
            def _(dve):
                for t in range(NT):
                    for kk in range(K0):
                        if t * K0 + kk:
                            dve.wait_ge(weighed, t * K0 + kk)
                        nc.vector.scalar_tensor_tensor(picked[:, :], r["rank"][:, t, :], r["slot8"][:, t, kk:kk + 1],
                                                       coef[:, t, :], ALU.is_equal, ALU.mult,
                                                       accum_out=wt[:, t, kk:kk + 1]).then_inc(weighed, 1)
                    dve.wait_ge(weighed, (t + 1) * K0)
                    dve.wait_ge(y_in[t % 2], (t // 2 + 1) * K0 * 16)
                    for kk in range(K0):
                        if kk:
                            dve.wait_ge(added, t * K0 + kk)
                        nc.vector.scalar_tensor_tensor(h[:, t, :], y[:, t % 2, kk, :], wt[:, t, kk:kk + 1], h[:, t, :],
                                                       ALU.mult, ALU.add).then_inc(added, 1)


def roll_attention(nc, a, k):
    h, xT = k["h"], k["xT"]
    ident = k["const"]("ident")
    PAIRS = B // 2
    CP = 2 * S
    BLK = 8
    CZ = T // BLK
    fwd = [k["const"]("fwd_re"), k["const"]("fwd_im")]
    inv = [k["const"]("inv_re"), k["const"]("inv_im")]
    with ExitStack() as st:
        sb = lambda n, s, d=fp32: k["sb"](f"ra_{n}", s, d, st)
        w_a = sb("w_a", [P, DC, H])
        w_v, w_o = sb("w_v", [P, DC, D]), sb("w_o", [P, DC, D])
        b_o = sb("b_o", [P, D])
        z = sb("z", [H, B, S])
        zpeak, zsum = sb("zpeak", [H, B]), sb("zsum", [H, B])
        zt = sb("zt", [S, B, H])
        zf = sb("zf", [NF, 2, B, H])
        aT = sb("aT", [P, DC, T])
        with ExitStack() as zs:
            pz = zs.enter_context(nc.psum_tensor("ra_pz", [P, 2, 512], fp32))
            pzt = zs.enter_context(nc.psum_tensor("ra_pzt", [P, 512], fp32))
            pzf = zs.enter_context(nc.psum_tensor("ra_pzf", [P, 2, 512], fp32))
            (w_in, logits, moved, chain, exped, normalised, turned, turn_moved, transformed, biased) = sems(
                nc, k, "raz", "w_in logits moved chain exped normalised turned turn_moved transformed biased")
            with nc.Block() as block:

                @block.sync
                def _(sp):
                    for dst, src in ((w_a, "w_a"), (w_v, "w_v"), (w_o, "w_o")):
                        sp.dma_start(dst[:, :, :], a[src]).then_inc(w_in, 16)
                    sp.dma_start(b_o[:, :], a["b_o"].broadcast_to([P, D])).then_inc(w_in, 16)

                @block.gpsimd
                def _(pool):
                    pool.wait_ge(w_in, 64)
                    for t in range(NT):
                        nc.gpsimd.tensor_tensor(h[:, t, :], h[:, t, :], b_o[:, :], ALU.add).then_inc(biased, 1)

                @block.tensor
                def _(pe):
                    pe.wait_ge(w_in, 64)
                    for i in range(BLK):
                        if i >= 2:
                            pe.wait_ge(moved, i - 1)
                        for c in range(DC):
                            mm = nc.tensor.matmul(pz[0:H, i % 2, 0:CZ], w_a[:, c, :], xT[:, c, i * CZ:(i + 1) * CZ],
                                                  start=(c == 0), stop=(c == DC - 1))
                        mm.then_inc(logits, 1)
                    pe.wait_ge(normalised, 1)
                    for b in range(B):
                        mm = nc.tensor.transpose(pzt[0:S, b * H:(b + 1) * H], z[:, b, :], ident[0:H, 0:H])
                    mm.then_inc(turned, 1)
                    pe.wait_ge(turn_moved, 1)
                    for part in range(2):
                        mm = nc.tensor.matmul(pzf[0:NF, part, :], fwd[part], zt[:, :, :].rearrange("s b m -> s (b m)"),
                                              start=True, stop=True)
                    mm.then_inc(transformed, 1)

                @block.scalar
                def _(act):
                    zflat = z[:, :, :].rearrange("m b s -> m (b s)")
                    for i in range(BLK):
                        act.wait_ge(logits, i + 1)
                        nc.scalar.activation(zflat[:, i * CZ:(i + 1) * CZ], pz[0:H, i % 2, 0:CZ], ACT.Copy,
                                             scale=float(HD) ** -0.5).then_inc(moved, 1)
                    act.wait_ge(chain, 2)
                    nc.scalar.activation(z[:, :, :], z[:, :, :], ACT.Exp).then_inc(exped, 1)

                @block.vector
                def _(dve):
                    done = [0]

                    def link(ins):
                        done[0] += 1
                        ins.then_inc(chain, 1)
                        dve.wait_ge(chain, done[0])

                    dve.wait_ge(moved, BLK)
                    link(nc.vector.tensor_reduce(zpeak[:, :], z[:, :, :], AX.X, ALU.max))
                    link(nc.vector.tensor_tensor(z[:, :, :], z[:, :, :], zpeak[:, :].unsqueeze(2).broadcast_to([H, B, S]),
                                                 ALU.subtract))
                    dve.wait_ge(exped, 1)
                    link(nc.vector.tensor_reduce(zsum[:, :], z[:, :, :], AX.X, ALU.add))
                    link(nc.vector.reciprocal(zsum[:, :], zsum[:, :]))
                    nc.vector.tensor_tensor(z[:, :, :], z[:, :, :], zsum[:, :].unsqueeze(2).broadcast_to([H, B, S]),
                                            ALU.mult).then_inc(normalised, 1)
                    dve.wait_ge(turned, 1)
                    nc.vector.tensor_copy(zt[:, :, :].rearrange("s b m -> s (b m)"), pzt[0:S, :]).then_inc(turn_moved, 1)
                    dve.wait_ge(transformed, 1)
                    link(nc.vector.tensor_copy(zf[:, :, :, :].rearrange("f r b m -> f r (b m)"), pzf[0:NF, :, :]))

        xb = sb("xb", [P, 2, DC, CP])
        v = sb("v", [S, 2, 2, D])
        term = sb("term", [NF, 2, 4, 2 * D])
        R = 4
        prod = sb("prod", [NF, R, 2, 2, D])
        with ExitStack() as vs:
            pv = vs.enter_context(nc.psum_tensor("ra_pv", [P, 2, 512], fp32))
            pf = vs.enter_context(nc.psum_tensor("ra_pf", [P, 2, 2, 512], fp32))
            po = vs.enter_context(nc.psum_tensor("ra_po", [P, 2, 512], fp32))
            (copied, valued, v_moved, transformed, terms, multiplied, differences, products, inverted, out_moved) = sems(
                nc, k, "rav", "copied valued v_moved transformed terms multiplied differences products inverted out_moved")
            with nc.Block() as block:

                def pairs(eng, body):
                    body(True, 0)
                    with eng.Fori(1, PAIRS // R, 1) as n:
                        body(False, n)

                @block.gpsimd
                def _(pool):
                    def copy(j, s, first):
                        if not first:
                            pool.wait_ge(valued, j - 1)
                        nc.gpsimd.tensor_copy(xb[:, s, :, :], xT[:, :, bass.ds(j * CP, CP)]).then_inc(copied, 1)

                    def body(first, n, last=False):
                        for slot in range(R):
                            j = n * R + slot
                            if not (last and slot == R - 1):
                                copy(j + 1, (slot + 1) % 2, first and slot == 0)
                            pool.wait_ge(terms, j + 1)
                            if not first:
                                pool.wait_ge(inverted, j - R + 1)
                            nc.gpsimd.tensor_tensor(prod[:, slot, 1, :, :].rearrange("f b n -> f (b n)"),
                                                    term[:, slot % 2, 2, :], term[:, slot % 2, 3, :], ALU.add)\
                                .then_inc(products, 1)

                    copy(0, 0, True)
                    body(True, 0)
                    with pool.Fori(1, PAIRS // R - 1, 1) as n:
                        body(False, n)
                    body(False, PAIRS // R - 1, True)

                @block.tensor
                def _(pe):
                    def values(j, s, b, early):
                        if b == 0:
                            pe.wait_ge(copied, j + 1)
                            if not early:
                                pe.wait_ge(v_moved, j - 1)
                        for c in range(DC):
                            mm = nc.tensor.matmul(pv[0:S, s, b * D:(b + 1) * D], xb[:, s, c, b * S:(b + 1) * S],
                                                  w_v[:, c, :], start=(c == 0), stop=(c == DC - 1))
                        if b == 1:
                            mm.then_inc(valued, 1)

                    def transform(j, s, part, early):
                        if part == 0:
                            pe.wait_ge(v_moved, j + 1)
                            if not early:
                                pe.wait_ge(multiplied, j - 1)
                        mm = nc.tensor.matmul(pf[0:NF, s, part, :], fwd[part],
                                              v[:, s, :, :].rearrange("s b n -> s (b n)"), start=True, stop=True)
                        if part == 1:
                            mm.then_inc(transformed, 1)

                    def invert(j, slot, c, b, early):
                        if c == 0 and b == 0:
                            pe.wait_ge(products, j + 1)
                            pe.wait_ge(differences, j + 1)
                            if not early:
                                pe.wait_ge(out_moved, j - 1)
                        for part in range(2):
                            mm = nc.tensor.matmul(po[:, slot % 2, (c * 2 + b) * S:(c * 2 + b + 1) * S],
                                                  prod[:, slot, part, b, c * P:(c + 1) * P], inv[part],
                                                  start=(part == 0), stop=(part == 1))
                        if c == 1 and b == 1:
                            mm.then_inc(inverted, 1)

                    def step(j, slot, back=True, early=False, inv_early=False, last=False):
                        for part in range(2):
                            transform(j, slot % 2, part, early)
                            if back:
                                invert(j - 2, (slot - 2) % R, 0, part, inv_early)
                        for b in range(2):
                            if not last:
                                values(j + 1, (slot + 1) % 2, b, early and slot == 0)
                            if back:
                                invert(j - 2, (slot - 2) % R, 1, b, inv_early)

                    for b in range(2):
                        values(0, 0, b, True)
                    for j in range(R):
                        step(j, j, back=j >= 2, early=j < 2, inv_early=j < 4)
                    with pe.Fori(1, PAIRS // R - 1, 1) as n:
                        for slot in range(R):
                            step(n * R + slot, slot)
                    for slot in range(R):
                        step(PAIRS - R + slot, slot, last=slot == R - 1)
                    for j in (PAIRS - 2, PAIRS - 1):
                        for c in range(DC):
                            for b in range(2):
                                invert(j, j % R, c, b, False)

                @block.scalar
                def _(act):
                    def move_out(j, slot):
                        act.wait_ge(inverted, j + 1)
                        nc.scalar.activation(aT[:, :, bass.ds(j * CP, CP)],
                                             po[:, slot % 2, 0:DC * CP].rearrange("p (c n) -> p c n", c=DC),
                                             ACT.Copy).then_inc(out_moved, 1)

                    def body(first, n):
                        for slot in range(R):
                            j = n * R + slot
                            act.wait_ge(valued, j + 1)
                            if not (first and slot < 2):
                                act.wait_ge(transformed, j - 1)
                            nc.scalar.activation(v[:, slot % 2, :, :].rearrange("s b n -> s (b n)"),
                                                 pv[0:S, slot % 2, :], ACT.Copy).then_inc(v_moved, 1)
                            if not (first and slot < 3):
                                move_out(j - 3, (slot - 3) % R)

                    pairs(act, body)
                    for j in range(PAIRS - 3, PAIRS):
                        move_out(j, j % R)

                @block.vector
                def _(dve):
                    def body(first, n):
                        for slot in range(R):
                            j, s = n * R + slot, slot % 2
                            dve.wait_ge(transformed, j + 1)
                            if not (first and slot < 2):
                                dve.wait_ge(products, j - 1)
                            for i, pv_, pz_ in ((2, 0, 1), (3, 1, 0), (0, 0, 0), (1, 1, 1)):
                                weights = zf[:, pz_, bass.ds(j * 2, 2), :].rearrange("f b m -> f (b m)")
                                mm = nc.vector.tensor_tensor(
                                    term[:, s, i, :].rearrange("f (m n) -> f m n", n=HD),
                                    pf[0:NF, s, pv_, :].rearrange("f (m n) -> f m n", n=HD),
                                    weights.unsqueeze(2).broadcast_to([NF, 2 * H, HD]), ALU.mult)
                                if i == 3:
                                    mm.then_inc(terms, 1)
                            mm.then_inc(multiplied, 1)
                            dve.wait_ge(multiplied, j + 1)
                            if not first:
                                dve.wait_ge(inverted, j - R + 1)
                            nc.vector.tensor_tensor(prod[:, slot, 0, :, :].rearrange("f b n -> f (b n)"),
                                                    term[:, s, 0, :], term[:, s, 1, :], ALU.subtract)\
                                .then_inc(differences, 1)
                    pairs(dve, body)

        project_out(nc, k, st, "ro", aT, w_o)


def mixture_1(nc, a, k):
    h, xn, xT = k["h"], k["xn"], k["xT"]
    with ExitStack() as st:
        sb = lambda n, s, d=fp32: k["sb"](f"m1_{n}", s, d, st)
        x_rows = nc.dram_tensor("m1_x_rows", (T, D), fp32).ap()
        y_rows = nc.dram_tensor("m1_y_rows", (SLOTS1 * P, D), fp32).ap()
        experts_dram = nc.dram_tensor("m1_tile_experts", (2, P), i32).ap()
        gate = sb("gate", [P, NT])
        ids = sb("ids", [P, SLOTS1], u32)
        tile_expert_row = sb("tile_expert_row", [1, 2 * P], i32)
        r = places(k, st, "m1", E1, 1, SLOTS1)
        w1 = sb("w1", [P, 2, DC, F1])
        w2 = sb("w2", [P, 2, FC1, D])
        with ExitStack() as rs:
            rb = lambda n, s, d=fp32: k["sb"](f"m1_{n}", s, d, rs)
            wr = rb("wr", [P, DC, E1])
            br = rb("br", [P, E1])
            logit = rb("logit", [P, NT, E1])
            peak = rb("peak", [P, NT])
            exps = rb("exps", [P, NT, E1])
            order = rb("order", [P, NT, E1])
            pcount = rs.enter_context(nc.psum_tensor("m1_pcount", [P, 1, 512], fp32))
            ptable = rs.enter_context(nc.psum_tensor("m1_ptable", [P, 512], fp32))
            (w_in, rows_out, logits, chain, shifted, exped, chosen_ready, set_up, ranks, ranks_out, totals, hot,
             hot_used, tabled, experts_ready, experts_out, experts_back) = sems(
                nc, k, "m1r", "w_in rows_out logits chain shifted exped chosen_ready set_up ranks ranks_out totals "
                "hot hot_used tabled experts_ready experts_out experts_back")
            with nc.Block() as block:

                @block.sync
                def _(sp):
                    sp.dma_start(wr[:, :, :], a["wr"]).then_inc(w_in, 16)
                    sp.dma_start(br[:, :], a["br"].broadcast_to([P, E1])).then_inc(w_in, 16)
                    sp.dma_start(x_rows.rearrange("(t p) d -> p t d", p=P), xn[:, :, :]).then_inc(rows_out, 16)
                    sp.wait_ge(experts_ready, 1)
                    sp.dma_start(experts_dram.rearrange("q p -> p q"), r["tile_expert_i"][:, :],
                                 allow_slow_non_contiguous=True).then_inc(experts_out, 16)
                    sp.wait_ge(experts_out, 16)
                    sp.dma_start(tile_expert_row[:, :], experts_dram.rearrange("(o q) p -> o (q p)", o=1))\
                        .then_inc(experts_back, 16)
                    sp.wait_ge(experts_back, 16)
                    sp.wait_ge(rows_out, 16)

                @block.gpsimd
                def _(pool):
                    nc.gpsimd.tensor_copy(r["before_b"][:, :], k["const"]("before")).then_inc(set_up, 1)
                    nc.gpsimd.memset(r["ones_b"][:, :], 1.0).then_inc(set_up, 1)
                    nc.gpsimd.tensor_copy(r["iota_h"][:, :], k["const"]("iota")).then_inc(set_up, 1)

                @block.scalar
                def _(act):
                    act.wait_ge(shifted, 1)
                    nc.scalar.activation(exps[:, :, :], logit[:, :, :], ACT.Exp).then_inc(exped, 1)

                @block.tensor
                def _(pe):
                    pe.wait_ge(w_in, 32)
                    for t in range(NT):
                        for c in range(DC):
                            mm = nc.tensor.matmul(pcount[:, 0, t * E1:(t + 1) * E1], xT[:, c, t * P:(t + 1) * P],
                                                  wr[:, c, :], start=(c == 0), stop=(c == DC - 1))
                    mm.then_inc(logits, 1)
                    pe.wait_ge(set_up, 3)
                    pe.wait_ge(chosen_ready, 1)
                    chosen = r["chosen_b"][:, :, :].rearrange("p t e -> p (t e)")
                    nc.tensor.matmul(pcount[:, 0, 0:NT * E1], r["before_b"][:, :], chosen, start=True, stop=True)\
                        .then_inc(ranks, 1)
                    pe.wait_ge(ranks_out, 1)
                    nc.tensor.matmul(pcount[:, 0, 0:NT * E1], r["ones_b"][:, :], chosen, start=True, stop=True)\
                        .then_inc(totals, 1)
                    gather_table(nc, pe, r, ptable, hot, hot_used, tabled)

                @block.vector
                def _(dve):
                    done = [0]

                    def link(ins):
                        done[0] += 1
                        ins.then_inc(chain, 1)
                        dve.wait_ge(chain, done[0])

                    vt = nc.vector.tensor_tensor
                    wide = lambda x: x[:, :].unsqueeze(2).broadcast_to([P, NT, E1])
                    dve.wait_ge(w_in, 32)
                    dve.wait_ge(logits, 1)
                    link(vt(logit[:, :, :], pcount[:, 0, 0:NT * E1].rearrange("p (t e) -> p t e", e=E1),
                            br[:, :].unsqueeze(1).broadcast_to([P, NT, E1]), ALU.add))
                    link(nc.vector.tensor_reduce(peak[:, :], logit[:, :, :], AX.X, ALU.max))
                    link(vt(order[:, :, :], logit[:, :, :], wide(peak), ALU.is_equal))
                    link(vt(order[:, :, :], order[:, :, :],
                            k["const"]("down_from").unsqueeze(1).broadcast_to([P, NT, E1]), ALU.mult))
                    vt(logit[:, :, :], logit[:, :, :], wide(peak), ALU.subtract).then_inc(shifted, 1)
                    dve.wait_ge(shifted, 1)
                    link(nc.vector.tensor_reduce(peak[:, :], order[:, :, :], AX.X, ALU.max))
                    vt(r["chosen_b"][:, :, :], order[:, :, :], wide(peak), ALU.is_equal).then_inc(chosen_ready, 1)
                    link(vt(r["chosen"][:, :, :], order[:, :, :], wide(peak), ALU.is_equal))
                    dve.wait_ge(exped, 1)
                    link(nc.vector.tensor_reduce(gate[:, :], exps[:, :, :], AX.X, ALU.add))
                    link(nc.vector.reciprocal(gate[:, :], gate[:, :]))
                    count_places(nc, dve, link, r, pcount, ranks, totals, ranks_out)
                    dve.wait_ge(set_up, 3)
                    one_hots(nc, dve, k, r, hot, hot_used)
                    tile_experts(nc, k, link, r, experts_ready)
                    dve.wait_ge(tabled, 1)
                    link(nc.vector.tensor_scalar(ids[:, :], ptable[:, 0:SLOTS1], float(TOK0), None, ALU.add))

        expert_tiles_1(nc, a, k, ids, tile_expert_row, x_rows, y_rows, w1, w2)
        combine_1(nc, k, r, gate, y_rows)


def expert_tiles_1(nc, a, k, ids, tile_expert_row, x_rows, y_rows, w1, w2):
    ident = k["const"]("ident")
    R = 2
    ROUNDS = SLOTS1 // R
    UNROLL = 5
    assert (ROUNDS - 2) % UNROLL == 0
    HB = 4
    with ExitStack() as es:
        sb = lambda n, s, d=fp32: k["sb"](f"x1_{n}", s, d, es)
        b1 = sb("b1", [P, R, FC1])
        b2 = sb("b2", [P, R, D])
        idx = sb("idx", [P, R], u32)
        x = sb("x", [P, R, D])
        xt = sb("xt", [P, R, D])
        hid = sb("hid", [P, R, FC1, P])
        y = sb("y", [P, R, D])
        pturn = es.enter_context(nc.psum_tensor("x1_pturn", [P, R, 512], fp32))
        pup = es.enter_context(nc.psum_tensor("x1_pup", [P, R, FC1 // HB, 512], fp32))
        pdown = es.enter_context(nc.psum_tensor("x1_pdown", [P, R, 512], fp32))
        (indexed, gathers, turned, turn_moved, up_done, hid_ready, down_done, down_moved) = sems(
            nc, k, "x1", "indexed gathers turned turn_moved up_done hid_ready down_done down_moved")
        w1_in = ring_sems(nc, k, "x1_w1_in", R)
        w2_in = ring_sems(nc, k, "x1_w2_in", R)
        x_in = ring_sems(nc, k, "x1_x_in", R)
        y_out = ring_sems(nc, k, "x1_y_out", R)
        with nc.Block() as block:

            def rounds(eng, body):
                body(True, 0)
                body(False, 1)
                with eng.Fori(2, ROUNDS - UNROLL + 1, UNROLL) as n:
                    for u in range(UNROLL):
                        body(False, n + u)

            @block.sync
            def _(sp):
                def load_up(e, s):
                    sp.dma_start(w1[:, s, :, :], a["w1"][bass.ds(e, 1), :, :, :].rearrange("o p c n -> (o p) c n"))\
                        .then_inc(w1_in[s], 16)
                    sp.dma_start(b1[:, s, :], a["b1"][bass.ds(e, 1), :, :].rearrange("o p c -> (o p) c"))\
                        .then_inc(w1_in[s], 16)

                def load_down(e, s):
                    sp.dma_start(w2[:, s, :, :], a["w2"][bass.ds(e, 1), :, :, :].rearrange("o p c n -> (o p) c n"))\
                        .then_inc(w2_in[s], 16)
                    sp.dma_start(b2[:, s, :], a["b2"][bass.ds(e, 1), :].broadcast_to([P, D])).then_inc(w2_in[s], 16)

                def body(first, n):
                    for s in range(R):
                        e = sp.value_load(tile_expert_row[0:1, bass.ds(s * ROUNDS + n, 1)], min_val=0, max_val=E1 - 1)
                        if not first:
                            sp.wait_ge(hid_ready, ((n - 1) * R + s + 1) * 2)
                        load_up(e, s)
                        if not first:
                            sp.wait_ge(down_moved, (n - 1) * R + s + 1)
                        load_down(e, s)
                rounds(sp, body)

            @block.gpsimd
            def _(pool):
                def take_ids(n, s):
                    nc.gpsimd.tensor_copy(idx[:, s:s + 1], ids[:, bass.ds(s * ROUNDS + n, 1)]).then_inc(indexed, 1)

                def body(first, n):
                    for s in range(R):
                        ahead, at = (n, s + 1) if s + 1 < R else (n + 1, 0)
                        if not first or s + 1 == R:
                            pool.wait_ge(x_in[at], ahead * 16)
                        take_ids(ahead, at)
                        if not first:
                            pool.wait_ge(turned, (n - 1) * R + s + 1)
                        pool.wait_ge(indexed, n * R + s + 1)
                        pool.sem_inc(gathers, 1)
                        nc.gpsimd.indirect_dma_start(x[:, s, :], None, x_rows,
                                                     bass.IndirectOffsetOnAxis(ap=idx[:, s:s + 1], axis=0))\
                            .then_inc(x_in[s], 16)
                take_ids(0, 0)
                rounds(pool, body)

            @block.tensor
            def _(pe):
                def turn(s, rnd, j, first):
                    pe.wait_ge(x_in[s], (rnd + 1) * 16)
                    if not first:
                        pe.wait_ge(turn_moved, j - 1)
                    for c in range(DC):
                        mm = nc.tensor.transpose(pturn[:, s, c * P:(c + 1) * P], x[:, s, c * P:(c + 1) * P], ident)
                    mm.then_inc(turned, 1)

                def up(s, rnd, j, first):
                    pe.wait_ge(w1_in[s], (rnd + 1) * 32)
                    pe.wait_ge(turn_moved, j + 1)
                    for half in range(FC1 // HB):
                        if not first:
                            pe.wait_ge(hid_ready, (j - 2) * 2 + half + 1)
                        for f in range(HB):
                            for c in range(DC):
                                mm = nc.tensor.matmul(pup[:, s, half, f * P:(f + 1) * P],
                                                      w1[:, s, c, (half * HB + f) * P:(half * HB + f + 1) * P],
                                                      xt[:, s, c * P:(c + 1) * P], start=(c == 0), stop=(c == DC - 1))
                        mm.then_inc(up_done, 1)

                def down(s, rnd, j, first):
                    pe.wait_ge(w2_in[s], (rnd + 1) * 32)
                    if not first:
                        pe.wait_ge(down_moved, j - 1)
                    for f in range(FC1):
                        if f % HB == 0:
                            pe.wait_ge(hid_ready, j * 2 + f // HB + 1)
                        mm = nc.tensor.matmul(pdown[:, s, 0:D], hid[:, s, f, :], w2[:, s, f, :],
                                              start=(f == 0), stop=(f == FC1 - 1))
                    mm.then_inc(down_done, 1)

                turn(0, 0, 0, True)
                up(0, 0, 0, True)
                turn(1, 0, 1, True)
                up(1, 0, 1, True)
                turn(0, 1, 2, False)
                down(0, 0, 0, True)
                up(0, 1, 2, False)
                turn(1, 1, 3, False)
                down(1, 0, 1, True)
                up(1, 1, 3, False)
                with pe.Fori(2, ROUNDS - UNROLL + 1, UNROLL) as first:
                    for n in (first + u for u in range(UNROLL)):
                        turn(0, n, n * 2, False)
                        down(0, n - 1, n * 2 - 2, False)
                        up(0, n, n * 2, False)
                        turn(1, n, n * 2 + 1, False)
                        down(1, n - 1, n * 2 - 1, False)
                        up(1, n, n * 2 + 1, False)
                down(0, ROUNDS - 1, SLOTS1 - 2, False)
                down(1, ROUNDS - 1, SLOTS1 - 1, False)

            @block.scalar
            def _(act):
                def body(first, n):
                    for s in range(R):
                        j = n * R + s
                        act.wait_ge(turned, j + 1)
                        if not first:
                            act.wait_ge(up_done, (j - R + 1) * 2)
                        nc.scalar.activation(xt[:, s, :], pturn[:, s, 0:D], ACT.Copy).then_inc(turn_moved, 1)
                        act.wait_ge(w1_in[s], (n + 1) * 32)
                        if not first:
                            act.wait_ge(down_done, j - R + 1)
                        for f in range(FC1):
                            if f % HB == 0:
                                act.wait_ge(up_done, j * 2 + f // HB + 1)
                            ins = nc.scalar.activation(hid[:, s, f, :], pup[:, s, f // HB, (f % HB) * P:(f % HB + 1) * P],
                                                       ACT.Gelu, bias=b1[:, s, f:f + 1])
                            if f % HB == HB - 1:
                                ins.then_inc(hid_ready, 1)
                        if not first:
                            store_y(n - 1, s)

                def store_y(n, s):
                    act.wait_ge(down_moved, n * R + s + 1)
                    act.dma_start(y_rows[bass.ds((s * ROUNDS + n) * P, P), :], y[:, s, :]).then_inc(y_out[s], 16)

                rounds(act, body)
                for s in range(R):
                    store_y(ROUNDS - 1, s)
                for s in range(R):
                    act.wait_ge(y_out[s], ROUNDS * 16)

            @block.vector
            def _(dve):
                def move_down(early, j, s, rnd):
                    dve.wait_ge(down_done, j + 1)
                    dve.wait_ge(w2_in[s], (rnd + 1) * 32)
                    if not early:
                        dve.wait_ge(y_out[s], rnd * 16)
                    nc.vector.tensor_tensor(y[:, s, :], pdown[:, s, 0:D], b2[:, s, :], ALU.add).then_inc(down_moved, 1)
                def body(first, n):
                    for s in range(R):
                        move_down(first, n * R + s, s, n)
                rounds(dve, body)



def combine_1(nc, k, r, gate, y_rows):
    h = k["h"]
    with ExitStack() as cs:
        sb = lambda n, s, d=fp32: k["sb"](f"c1_{n}", s, d, cs)
        idx = sb("idx", [P, NT], u32)
        y = sb("y", [P, NT, D])
        indexed, added = sems(nc, k, "c1", "indexed added")
        y_in = ring_sems(nc, k, "c1_y_in", 4)
        with nc.Block() as block:

            @block.gpsimd
            def _(pool):
                nc.gpsimd.tensor_copy(idx[:, :], r["slot"][:, :, 0]).then_inc(indexed, 1)
                pool.wait_ge(indexed, 1)
                for t in range(NT):
                    if t >= 4:
                        pool.wait_ge(added, t - 3)
                    nc.gpsimd.indirect_dma_start(y[:, t, :], None, y_rows,
                                                 bass.IndirectOffsetOnAxis(ap=idx[:, t:t + 1], axis=0))\
                        .then_inc(y_in[t % 4], 16)

            @block.vector
            def _(dve):
                for t in range(NT):
                    dve.wait_ge(y_in[t % 4], (t // 4 + 1) * 16)
                    nc.vector.scalar_tensor_tensor(h[:, t, :], y[:, t, :], gate[:, t:t + 1], h[:, t, :],
                                                   ALU.mult, ALU.add).then_inc(added, 1)


_INPUTS = ["patches", "txt", "tok_w", "tok_b", "wq", "wk", "wv", "wo", "bq", "bk", "bv", "bo",
           "router", "e_bias", "experts0", "shared_up", "shared_down",
           "w_a", "w_v", "w_o", "b_o", "w1", "b1", "w2", "b2", "wr", "br", "consts"]


def layout(np, x, txt, L0_tok_W, L0_tok_b, L0_attn_Wq, L0_attn_bq, L0_attn_Wk, L0_attn_bk, L0_attn_Wv, L0_attn_bv,
           L0_attn_Wo, L0_attn_bo, L0_ffn_router_w, L0_ffn_e_bias, L0_ffn_Wg, L0_ffn_Wu, L0_ffn_Wd,
           L0_ffn_SWg, L0_ffn_SWu, L0_ffn_SWd, L1_attn_W_A, L1_attn_W_V, L1_attn_W_O, L1_attn_b_O,
           L1_ffn_W1, L1_ffn_b1, L1_ffn_W2, L1_ffn_b2, L1_ffn_Wr, L1_ffn_br):
    def rows(w):
        w = np.asarray(w)
        return w.reshape(-1, P, w.shape[-1]).transpose(1, 0, 2)

    def cols(v):
        return np.asarray(v).reshape(-1, P).T

    img = np.asarray(x).reshape(B, 3, 6, 16, 6, 16).transpose(3, 5, 1, 0, 2, 4).reshape(PIN, B * NPATCH)
    g = np.asarray(L0_ffn_Wg).reshape(E0, DC, P, I0)
    u = np.asarray(L0_ffn_Wu).reshape(E0, DC, P, I0)
    experts0 = np.concatenate([g[:, 0], g[:, 1], u[:, 0], u[:, 1], np.asarray(L0_ffn_Wd)], axis=2)
    return {
        "patches": rows(img),
        "txt": rows(np.asarray(txt).reshape(B * NTXT, D).T),
        "tok_w": rows(np.asarray(L0_tok_W).T), "tok_b": cols(L0_tok_b),
        "wq": rows(L0_attn_Wq), "wk": rows(L0_attn_Wk), "wv": rows(L0_attn_Wv), "wo": rows(L0_attn_Wo),
        "bq": cols(L0_attn_bq), "bk": cols(L0_attn_bk), "bv": cols(L0_attn_bv), "bo": np.asarray(L0_attn_bo)[None, :],
        "router": rows(np.asarray(L0_ffn_router_w).T), "e_bias": np.asarray(L0_ffn_e_bias)[None, :],
        "experts0": experts0,
        "shared_up": np.concatenate([rows(L0_ffn_SWg), rows(L0_ffn_SWu)], axis=2), "shared_down": rows(L0_ffn_SWd),
        "w_a": rows(np.asarray(L1_attn_W_A).T), "w_v": rows(np.asarray(L1_attn_W_V).T),
        "w_o": rows(np.asarray(L1_attn_W_O).T), "b_o": np.asarray(L1_attn_b_O)[None, :],
        "w1": np.asarray(L1_ffn_W1).reshape(E1, DC, P, F1).transpose(0, 2, 1, 3),
        "b1": np.asarray(L1_ffn_b1).reshape(E1, FC1, P).transpose(0, 2, 1),
        "w2": np.asarray(L1_ffn_W2).reshape(E1, FC1, P, D).transpose(0, 2, 1, 3),
        "b2": np.asarray(L1_ffn_b2),
        "wr": rows(L1_ffn_Wr), "br": np.asarray(L1_ffn_br)[None, :],
        "consts": constants()[0],
    }


def kernel(**inputs):
    import concourse.bacc as bacc
    from concourse.bass_utils import run_bass_kernel_spmd

    nc = bacc.Bacc("TRN2", target_bir_lowering=False, num_devices=1)
    arrays, handles = {}, {}
    laid = layout(np, **inputs)
    for name in _INPUTS:
        v = np.ascontiguousarray(laid[name])
        arrays[f"in_{name}"] = v
        handles[name] = nc.dram_tensor(f"in_{name}", v.shape, mybir.dt.from_np(v.dtype), kind="ExternalInput").ap()
    out = nc.dram_tensor("out_h", (T, D), fp32, kind="ExternalOutput").ap()
    early_fusion(nc, handles, out)
    r = run_bass_kernel_spmd(nc, [arrays], core_ids=[0])
    return r.results[0]["out_h"].reshape(B, S, D)
```
